# Optimizing a Trainium2 kernel written in Bass

```python
import numpy as np
import jax
import jax.numpy as jnp

def _softmax(x, axis=-1):
    return jax.nn.softmax(x, axis=axis)

def _gelu(x):
    return jax.nn.gelu(x, approximate=True)

def _silu(x):
    return jax.nn.silu(x)

def _sigmoid(x):
    return jax.nn.sigmoid(x)

def _layernorm(x, axis=-1, eps=1e-05):
    m = jnp.mean(x, axis=axis, keepdims=True)
    v = jnp.var(x, axis=axis, keepdims=True)
    return (x - m) / jnp.sqrt(v + eps)

def _scatter_add(tgt, idx, src, axis=0):
    return tgt.at[idx].add(src)

def _segment_sum(src, seg, n):
    return jax.ops.segment_sum(src, seg, n)
kernel_name = 'mk_macaron_d1_jaxref_r4_9f8d67'

def setup_inputs(seed: int=0):
    np.random.seed(seed)
    _w = jnp.asarray

    def _L0_attn_setup():
        import math
        import jax, jax.numpy as jnp
        import numpy as np
        N_HEAD = 16

        def _rope_cos_sin(l, head_dim):
            scale = jnp.arange(0, head_dim, 2, dtype=jnp.float32)[:head_dim // 2]
            freqs = 1.0 / 10000.0 ** scale
            angles = jnp.arange(l, dtype=jnp.float32)[:, None] * freqs[None, :]
            return (jnp.cos(angles), jnp.sin(angles))

        def _rope_apply(x, cos, sin):
            b, l, h, hd = x.shape
            xp = x.astype(jnp.float32).reshape(b, l, h, hd // 2, 2)
            xr, xi = (xp[..., 0], xp[..., 1])
            c = cos[None, :, None, :]
            s = sin[None, :, None, :]
            out_r = xr * c - xi * s
            out_i = xr * s + xi * c
            out = jnp.stack([out_r, out_i], axis=-1).reshape(b, l, h, hd)
            return out.astype(x.dtype)
        key = jax.random.key(seed)
        ks = jax.random.split(key, 9)
        b, l, d = (2, 512, 256)
        sc = 1.0 / math.sqrt(d)
        inp = {'x': jax.random.normal(ks[0], (b, l, d), dtype=jnp.float32), 'Wq': jax.random.normal(ks[1], (d, d), dtype=jnp.float32) * sc, 'bq': jnp.zeros((d,), dtype=jnp.float32), 'Wk': jax.random.normal(ks[2], (d, d), dtype=jnp.float32) * sc, 'bk': jnp.zeros((d,), dtype=jnp.float32), 'Wv': jax.random.normal(ks[3], (d, d), dtype=jnp.float32) * sc, 'bv': jnp.zeros((d,), dtype=jnp.float32), 'Wo': jax.random.normal(ks[4], (d, d), dtype=jnp.float32) * sc, 'bo': jnp.zeros((d,), dtype=jnp.float32)}
        return inp
    _L0_attn_in = _L0_attn_setup()

    def _L0_ffn_setup():
        import jax, jax.numpy as jnp
        import numpy as np
        B, S, H, E, I, K = (2, 512, 256, 8, 256, 2)
        ALPHA, LIMIT = (1.702, 7.0)
        key = jax.random.key(seed)
        ks = jax.random.split(key, 5)
        sc = 0.02
        return {'hidden_states': jax.random.normal(ks[0], (B, S, H), jnp.float32), 'router_weight': jax.random.normal(ks[1], (H, E), jnp.float32) * sc, 'gate_up_proj': jax.random.normal(ks[2], (E, H, 2 * I), jnp.float32) * sc, 'gate_up_proj_bias': jnp.zeros((E, 2 * I), jnp.float32), 'down_proj': jax.random.normal(ks[3], (E, I, H), jnp.float32) * sc, 'down_proj_bias': jnp.zeros((E, H), jnp.float32)}
    _L0_ffn_in = _L0_ffn_setup()
    _d = {'L0_attn_x': _L0_attn_in['x'], 'L0_attn_Wq': _L0_attn_in['Wq'], 'L0_attn_bq': _L0_attn_in['bq'], 'L0_attn_Wk': _L0_attn_in['Wk'], 'L0_attn_bk': _L0_attn_in['bk'], 'L0_attn_Wv': _L0_attn_in['Wv'], 'L0_attn_bv': _L0_attn_in['bv'], 'L0_attn_Wo': _L0_attn_in['Wo'], 'L0_attn_bo': _L0_attn_in['bo'], 'L0_ffn_router_weight': _L0_ffn_in['router_weight'], 'L0_ffn_gate_up_proj': _L0_ffn_in['gate_up_proj'], 'L0_ffn_gate_up_proj_bias': _L0_ffn_in['gate_up_proj_bias'], 'L0_ffn_down_proj': _L0_ffn_in['down_proj'], 'L0_ffn_down_proj_bias': _L0_ffn_in['down_proj_bias']}
    _x0 = _d['L0_attn_x']
    _d['L0_attn_x'] = jax.random.normal(jax.random.fold_in(jax.random.key(seed), 1), (1, 4096, 256), dtype=_x0.dtype)
    del _x0
    return _d

def reference(L0_attn_x, L0_attn_Wq, L0_attn_bq, L0_attn_Wk, L0_attn_bk, L0_attn_Wv, L0_attn_bv, L0_attn_Wo, L0_attn_bo, L0_ffn_router_weight, L0_ffn_gate_up_proj, L0_ffn_gate_up_proj_bias, L0_ffn_down_proj, L0_ffn_down_proj_bias):

    def _L0_attn_ref(x, Wq, bq, Wk, bk, Wv, bv, Wo, bo):
        import math
        import jax, jax.numpy as jnp
        import numpy as np
        N_HEAD = 16

        def _rope_cos_sin(l, head_dim):
            scale = jnp.arange(0, head_dim, 2, dtype=jnp.float32)[:head_dim // 2]
            freqs = 1.0 / 10000.0 ** scale
            angles = jnp.arange(l, dtype=jnp.float32)[:, None] * freqs[None, :]
            return (jnp.cos(angles), jnp.sin(angles))

        def _rope_apply(x, cos, sin):
            b, l, h, hd = x.shape
            xp = x.astype(jnp.float32).reshape(b, l, h, hd // 2, 2)
            xr, xi = (xp[..., 0], xp[..., 1])
            c = cos[None, :, None, :]
            s = sin[None, :, None, :]
            out_r = xr * c - xi * s
            out_i = xr * s + xi * c
            out = jnp.stack([out_r, out_i], axis=-1).reshape(b, l, h, hd)
            return out.astype(x.dtype)
        b, l, d = x.shape
        h = N_HEAD
        hd = d // h
        q = (x @ Wq + bq).reshape(b, l, h, hd)
        k = (x @ Wk + bk).reshape(b, l, h, hd)
        v = (x @ Wv + bv).reshape(b, l, h, hd)
        cos, sin = _rope_cos_sin(l, hd)
        q = _rope_apply(q, cos, sin)
        k = _rope_apply(k, cos, sin)
        score = jnp.einsum('blhd,bmhd->bhlm', q, k) / math.sqrt(hd)
        ctx = jnp.einsum('bhlm,bmhd->blhd', score, v).reshape(b, l, d)
        return ctx @ Wo + bo

    def _L0_ffn_ref(hidden_states, router_weight, gate_up_proj, gate_up_proj_bias, down_proj, down_proj_bias):
        import jax, jax.numpy as jnp
        import numpy as np
        B, S, H, E, I, K = (2, 512, 256, 8, 256, 2)
        ALPHA, LIMIT = (1.702, 7.0)
        Bt, St, Ht = hidden_states.shape
        x = hidden_states.reshape(-1, Ht)
        T = x.shape[0]
        logits = x @ router_weight
        top_vals, top_idx = jax.lax.top_k(logits, K)
        scores = jax.nn.softmax(top_vals, axis=-1)
        w = jnp.zeros((T, E), x.dtype).at[jnp.arange(T)[:, None], top_idx].set(scores)
        gu = jnp.einsum('th,ehf->tef', x, gate_up_proj) + gate_up_proj_bias
        gate = gu[..., ::2]
        up = gu[..., 1::2]
        gate = jnp.minimum(gate, LIMIT)
        up = jnp.clip(up, -LIMIT, LIMIT)
        glu = gate * jax.nn.sigmoid(gate * ALPHA)
        act = (up + 1.0) * glu
        down = jnp.einsum('tei,eih->teh', act, down_proj) + down_proj_bias
        out = jnp.einsum('te,teh->th', w, down)
        return out.reshape(Bt, St, Ht)
    x = L0_attn_x
    x = x + 0.5 * _L0_ffn_ref(_layernorm(x, axis=-1), L0_ffn_router_weight, L0_ffn_gate_up_proj, L0_ffn_gate_up_proj_bias, L0_ffn_down_proj, L0_ffn_down_proj_bias)
    x = x + _L0_attn_ref(_layernorm(x, axis=-1), L0_attn_Wq, L0_attn_bq, L0_attn_Wk, L0_attn_bk, L0_attn_Wv, L0_attn_bv, L0_attn_Wo, L0_attn_bo)
    x = x + 0.5 * _L0_ffn_ref(_layernorm(x, axis=-1), L0_ffn_router_weight, L0_ffn_gate_up_proj, L0_ffn_gate_up_proj_bias, L0_ffn_down_proj, L0_ffn_down_proj_bias)
    return x

_drawn_inputs = setup_inputs


def setup_inputs(seed=0):
    import zlib

    import numpy as np

    out = dict(_drawn_inputs(seed))
    spreads = {'L0_attn_bq': (0.0, 0.1),
     'L0_attn_bk': (0.0, 0.1),
     'L0_attn_bv': (0.0, 0.1),
     'L0_attn_bo': (0.0, 0.8),
     'L0_ffn_gate_up_proj_bias': (0.0, 0.685),
     'L0_ffn_down_proj_bias': (0.0, 0.1)}
    factors = {}
    for name, (base, spread) in spreads.items():
        noise = np.random.default_rng([zlib.crc32(name.encode()), seed]).standard_normal(out[name].shape)
        drawn = base * np.exp(spread * noise) if base else spread * noise
        out[name] = jnp.asarray(drawn.astype(out[name].dtype))
    for name, factor in factors.items():
        out[name] = (out[name] * factor).astype(out[name].dtype)
    return out
```

```python
from contextlib import ExitStack

import concourse.bass as bass
from concourse import mybir

ALU = mybir.AluOpType
ACT = mybir.ActivationFunctionType
AX = mybir.AxisListType
F32 = mybir.dt.float32
F32R = mybir.dt.float32r
BF16 = mybir.dt.bfloat16
I32 = mybir.dt.int32
U32 = mybir.dt.uint32

P = 128
T, H = 4096, 256
NT = T // P
NG = NT // 2
KC = H // P
E, I = 8, 256
F = 2 * I
TOPK = 2
HEADS, HD = 16, 16
ROT = 5
NQ = TOPK * NT
NS = T * TOPK // P + E
NP = NS // 2
QC = 8
NQC = NQ // QC
PAD = 16
LIMIT, ALPHA = 7.0, 1.702
EPS = 1e-5
GLU_LIMIT = 6.9999536
MASKED = -3.0e38
SKIP = 16384.0

C_ID, C_UP, C_BLK = 0, P, 2 * P
C_COS = 3 * P
C_SIN = C_COS + NT
C_P = C_SIN + NT * ROT
C_E = C_P + 1
NCONST = C_E + E

B_UP, B_DN = 0, E * F
B_QK = B_DN + E * H
B_O = B_QK + 2 * H
NB = B_O + H

WORK = 8192


def wait(eng, sem, n):
    if not (isinstance(n, int) and n <= 0):
        eng.wait_ge(sem, n)


def repeat(eng, count, body):
    body(0)
    with eng.Fori(1, count) as it:
        body(it)


class Steps:

    def __init__(self, eng, sem, passed):
        self.eng, self.sem, self.passed, self.n, self.done_in_body = eng, sem, passed, 0, 0

    def hold(self):
        self.eng.sem_inc(self.passed, 1)

    def done(self, ins):
        self.n = self.n + 1
        self.done_in_body += 1
        ins.then_inc(self.sem, 1)
        self.eng.wait_ge(self.sem, self.n)

    def loop(self, count, per, body):
        base = self.n
        body(0)
        with self.eng.Fori(1, count) as it:
            self.n, self.done_in_body = base + it * per, 0
            body(it)
            assert self.done_in_body == per, self.done_in_body
        self.n = base + count * per


def build(nc, x, Wq, bq, Wk, bk, Wv, bv, Wo, bo, Wr, Wup, bup, Wdn, bdn, consts, out):
    ctx = ExitStack()

    def sb(name, shape, dt):
        return ctx.enter_context(nc.sbuf_tensor(name, shape, dt))

    def sem(name):
        return ctx.enter_context(nc.semaphore(name))

    def scratch(name, shape, dt=F32):
        return nc.dram_tensor(name, shape, dt).ap()

    with ctx:
        xn_dram = [scratch(f"xn_dram{n}", [T, H]) for n in range(2)]
        y_dram = [scratch(f"y_dram{n}", [T * TOPK, H]) for n in range(2)]
        q_dram = scratch("q_dram", [P, NT, H])
        bias_dram = scratch("bias_dram", [3, NB], BF16)

        xs = sb("xs", [P, NT, H], F32)
        up_w = [sb(f"up_{h}", [P, KC, E, F], F32R) for h in ("hi", "lo")]
        dn_w = [sb(f"dn_{h}", [P, KC, E, H], F32R) for h in ("hi", "lo")]
        qk_w = [sb(f"qk_{h}", [P, KC, 2 * H], F32R) for h in ("hi", "lo")]
        wv = sb("wv", [P, KC, H], F32)
        wo = sb("wo", [P, KC, H], F32)
        wr = sb("wr", [P, KC, E], F32)
        bvrow = sb("bvrow", [1, H], F32)
        biases = sb("biases", [P, NB], BF16)
        xT = [sb(f"xT_{h}", [P, 2, 2, KC, P], F32R) for h in ("hi", "lo")]
        aT = [sb(f"aT_{h}", [P, 2, KC, P], F32R) for h in ("hi", "lo")]
        xn1 = [sb(f"xn1_{h}", [P, 2, H + 2], F32R) for h in ("hi", "lo")]
        cst = sb("cst", [P, NCONST], F32)
        ones = sb("ones", [P, P], BF16)
        upper = sb("upper", [P, P], BF16)
        gate = sb("gate", [P, TOPK, NT], F32)
        gidx = sb("gidx", [P, NS], U32)
        sidx = sb("sidx", [P, NS], U32)
        gslot = sb("gslot", [P, 2, 2], U32)
        sslot = sb("sslot", [P, 2, 2], U32)
        expert = sb("expert", [1, NS], I32)
        small = sb("small", [P, 48], F32)
        bst = sb("bst", [P, 2, 6], F32)
        sbmv = sb("sbmv", [P, 8], F32)
        work = sb("work", [P, WORK], F32)
        ps = ctx.enter_context(nc.psum_tensor("ps", [P, 8, 512], F32))

        ident = cst[:, C_ID:C_ID + P]

        def area(at, *shape, dt=F32):
            n = 1
            for d in shape:
                n *= d
            words = n if dt in (F32, U32, I32) else n // 2
            assert at + words <= WORK
            v = work[:, at:at + words]
            if dt is not F32:
                v = v.bitcast(dt)
            names = "abcd"[:len(shape)]
            if len(shape) == 1:
                return v
            return v.rearrange(f"p ({' '.join(names)}) -> p {' '.join(names)}",
                               **dict(zip(names[1:], shape[1:])))

        raw = area(3136, 2, 1536)
        iotaS = area(2048, P, QC, dt=BF16)
        iotaJ = area(2560, NS, QC, dt=BF16)
        qnum = area(2848, NS, QC, dt=BF16)
        xn_r = area(0, 2, 2, H)
        xTf = area(1024, 2, 2, KC, P)
        xg = area(0, 2, 2, H)
        glu = area(1024, 2, 2, I)
        upv = area(2048, 2, I)
        act_v = area(2560, 2, 2, I)
        ysb = area(3584, 2, 2, H)
        ybuf = area(0, 2, 2, TOPK, H)
        xn_a = area(2048, 2, 2, H)
        qk = area(3072, 2, 2, 2 * H)
        rotr = area(5120, 2, 2 * HEADS, ROT)
        roti = area(5440, 2, 2 * HEADS, ROT)
        gsb = area(0, KC, H + 2)
        gT = area(1024, KC, H)
        ksT = area(2048, H)
        sT = area(2560, KC, P)
        qin = area(4096, 2, 2, H)
        bstage = area(6208, 54)
        bparts = area(6272, 3, 54, dt=BF16)
        bres = area(6400, 54)
        iint = area(6464, 2 * 576, dt=I32)

        x_loaded = [sem(f"x_loaded{c}") for c in range(4)]
        consts_loaded = sem("consts_loaded")
        small_loaded = sem("small_loaded")
        raw_loaded = [sem(f"raw_loaded{b}") for b in range(2)]
        raw_hi = sem("raw_hi")
        raw_lo = sem("raw_lo")
        bias_loaded = sem("bias_loaded")
        bias_split = sem("bias_split")
        bias_stored = sem("bias_stored")
        bias_ready = sem("bias_ready")
        bias_zeroed = sem("bias_zeroed")
        consts_made = sem("consts_made")
        iotas_made = sem("iotas_made")
        dve_step = sem("dve_step")
        pool_step = sem("pool_step")
        pool_passed = sem("pool_passed")
        dve_passed = sem("dve_passed")

        class Layer:

            def __init__(self, n):
                s = lambda name: sem(f"{name}{n}")
                self.var, self.sd, self.xn = s("var"), s("sd"), s("xn")
                self.xn_stored = [s("xn_stored_a"), s("xn_stored_b")]
                self.xn_T, self.xn_Tsb, self.logits = s("xn_T"), s("xn_Tsb"), s("logits")
                self.mask, self.prefix, self.gap = s("mask"), s("prefix"), s("gap")
                self.gates, self.hot, self.hot_used = s("gates"), s("hot"), s("hot_used")
                self.slots, self.routed = s("slots"), s("routed")
                self.gathered = [s("gathered_a"), s("gathered_b")]
                self.scattered = [s("scattered_a"), s("scattered_b")]
                self.x_T, self.x_hi, self.x_lo = s("x_T"), s("x_hi"), s("x_lo")
                self.gu, self.glu, self.act, self.upd = s("gu"), s("glu"), s("act"), s("upd")
                self.a_T, self.a_hi, self.a_lo = s("a_T"), s("a_hi"), s("a_lo")
                self.y_ps, self.y_sb = s("y_ps"), s("y_sb")
                self.y_loaded = [s("y_loaded_a"), s("y_loaded_b")]
                self.y_used = s("y_used")

        L = [Layer(0), Layer(1)]
        A = Layer(2)
        xn_hi, xn_lo = sem("xn_hi"), sem("xn_lo")
        qk_ps, qk_sb, rot_parts, rot_done = sem("qk_ps"), sem("qk_sb"), sem("rot_parts"), sem("rot_done")
        k_hi, k_lo, g_used = sem("k_hi"), sem("k_lo"), sem("g_used")
        q_stored = [sem("q_stored_a"), sem("q_stored_b")]
        q_loaded = [sem("q_loaded_a"), sem("q_loaded_b")]
        mid_pe, mid_dve, m_hi, m_lo = sem("mid_pe"), sem("mid_dve"), sem("m_hi"), sem("m_lo")
        q_T, q_hi, q_lo, o_ps, x_done = sem("q_T"), sem("q_hi"), sem("q_lo"), sem("o_ps"), sem("x_done")
        out_ready, out_stored = sem("out_ready"), sem("out_stored")

        block = ctx.enter_context(nc.Block())
        x_v = x.rearrange("b (p i) h -> p (b i) h", p=P)
        out_v = out.rearrange("b (p i) h -> p (b i) h", p=P)
        xn_v = [d.rearrange("(p i) h -> p i h", p=P) for d in xn_dram]
        y_v = [d.rearrange("(p i k) h -> p i k h", p=P, k=TOPK) for d in y_dram]

        def pair(v, g):
            return v[:, bass.ds(g * 2, 2)]

        def hot(b):
            at = 3136 + b * 1376
            return area(at, P, QC, dt=BF16), area(at + 512, NS, QC, dt=BF16), area(at + 800, NS, QC, dt=BF16)

        @block.sync
        def _(sp):
            sp.dma_start(cst[:, :], consts).then_inc(consts_loaded, 16)
            for c in range(4):
                sp.dma_start(xs[:, 8 * c:8 * c + 8, :], x_v[:, 8 * c:8 * c + 8, :]).then_inc(x_loaded[c], 16)

            def store_xn(n, g, b):
                sp.wait_ge(L[n].xn, g + 1)
                sp.dma_start(pair(xn_v[n], g), xn_r[:, b]).then_inc(L[n].xn_stored[b], 16)

            def body(it):
                for b in range(2):
                    store_xn(0, it * 2 + b, b)
            repeat(sp, NG // 2, body)

            def wait_scattered(n):
                for b in range(2):
                    sp.wait_ge(L[n].scattered[b], 32 * (NP // 2))

            wait_scattered(0)
            for b in range(2):
                sp.dma_start(ybuf[:, b], pair(y_v[0], b)).then_inc(L[0].y_loaded[b], 16)

            def store_q(g, b):
                sp.wait_ge(rot_done, g + 1)
                sp.dma_start(pair(q_dram, g), qk[:, b, :, 0:H]).then_inc(q_stored[b], 16)

            def first_pass(g, b, more):
                if more:
                    sp.wait_ge(L[0].y_used, g + 1)
                    sp.dma_start(ybuf[:, b], pair(y_v[0], g + 2)).then_inc(L[0].y_loaded[b], 16)
                store_q(g, b)

            def body(it):
                for b in range(2):
                    first_pass(it * 2 + b, b, True)
            repeat(sp, NG // 2 - 1, body)
            for b in range(2):
                first_pass(NG - 2 + b, b, False)

            for b in range(2):
                sp.wait_ge(q_stored[b], 16 * (NG // 2))
            sp.wait_ge(k_lo, NG)
            for b in range(2):
                sp.dma_start(qin[:, b], pair(q_dram, b)).then_inc(q_loaded[b], 16)

            def second_pass(g, b, more):
                if more:
                    sp.wait_ge(q_T, g + 1)
                    sp.dma_start(qin[:, b], pair(q_dram, g + 2)).then_inc(q_loaded[b], 16)
                store_xn(1, g, b)

            def body(it):
                for b in range(2):
                    second_pass(it * 2 + b, b, True)
            repeat(sp, NG // 2 - 1, body)
            for b in range(2):
                second_pass(NG - 2 + b, b, False)

            wait_scattered(1)
            for b in range(2):
                sp.dma_start(ybuf[:, b], pair(y_v[1], b)).then_inc(L[1].y_loaded[b], 16)

            def finish(g, b, more):
                sp.wait_ge(L[1].y_used, g + 1)
                sp.dma_start(pair(out_v, g), pair(xs, g)).then_inc(out_stored, 16)
                if more:
                    sp.dma_start(ybuf[:, b], pair(y_v[1], g + 2)).then_inc(L[1].y_loaded[b], 16)

            def body(it):
                for b in range(2):
                    finish(it * 2 + b, b, True)
            repeat(sp, NG // 2 - 1, body)
            for b in range(2):
                finish(NG - 2 + b, b, False)
            sp.wait_ge(out_stored, 16 * NG)

        @block.gpsimd
        def _(pool):
            st = Steps(pool, pool_step, pool_passed)
            pool.dma_start(wr[:, :, :], Wr.rearrange("(c p) e -> p c e", p=P)).then_inc(small_loaded, 16)
            pool.dma_start(wv[:, :, :], Wv.rearrange("(c p) o -> p c o", p=P)).then_inc(small_loaded, 16)
            pool.dma_start(wo[:, :, :], Wo.rearrange("(c p) o -> p c o", p=P)).then_inc(small_loaded, 16)
            pool.dma_start(bvrow[:, :], bv.rearrange("(a o) -> a o", a=1)).then_inc(small_loaded, 16)

            def make_iotas():
                for k, (dst, n, pattern, base) in enumerate((
                        (iotaS, P, [[1, P // 2], [0, QC]], 0),
                        (iotaS, P, [[1, P // 2], [0, QC]], P // 2),
                        (iotaJ, NS, [[1, NS], [0, QC]], 0), (qnum, NS, [[0, NS], [1, QC]], 1))):
                    n2 = pattern[0][1]
                    st.done(nc.gpsimd.iota(iint[:, 0:n2 * QC], pattern=pattern, base=base, channel_multiplier=0))
                    d = dst[:, base:base + n2, :] if n == P else dst[:, :, :]
                    st.done(nc.gpsimd.tensor_copy(d, iint[:, 0:n2 * QC].rearrange("p (a b) -> p a b", b=QC)))

            make_iotas()
            nc.gpsimd.memset(biases[:, :], 0.0).then_inc(bias_zeroed, 1)
            pool.sem_inc(iotas_made, 1)

            def low(c, b, parts):
                pool.wait_ge(raw_hi, c + 1)
                for j, (dst, src, hi) in enumerate(parts):
                    ins = nc.gpsimd.tensor_tensor(dst, src, hi.bitcast(F32), ALU.subtract)
                ins.then_inc(raw_lo, 1)

            def expert_parts(e, b, h):
                u, d = raw[:, b, 0:KC * F], raw[:, b, KC * F:KC * (F + H)]
                return ((up_w[h][:, :, bass.ds(e, 1), :].rearrange("p c a f -> p c (a f)"),
                         u.rearrange("p (c f) -> p c f", c=KC)),
                        (dn_w[h][:, :, bass.ds(e, 1), :].rearrange("p c a f -> p c (a f)"),
                         d.rearrange("p (c f) -> p c f", c=KC)))

            def body(it):
                for b in range(2):
                    e = it * 2 + b
                    low(e, b, [(lo, src, hi) for (lo, src), (hi, _) in
                               zip(expert_parts(e, b, 1), expert_parts(e, b, 0))])
            repeat(pool, E // 2, body)
            low(E, 0, [(qk_w[1][:, :, :], raw[:, 0, 0:KC * 2 * H].rearrange("p (c f) -> p c f", c=KC),
                        qk_w[0][:, :, :])])

            def experts(n):
                l = L[n]
                for b in range(2):
                    pool.wait_ge(l.xn_stored[b], 16 * (NG // 2))
                pool.wait_ge(l.routed, 1)

                def gather(s, b):
                    st.hold()
                    st.done(nc.gpsimd.tensor_copy(gslot[:, b, :], gidx[:, bass.ds(s * 2, 2)]))
                    st.hold()
                    for u in range(2):
                        pool.indirect_dma_start(xg[:, b, u, :], None, xn_dram[n],
                                                bass.IndirectOffsetOnAxis(ap=gslot[:, b, u:u + 1], axis=0)
                                                ).then_inc(l.gathered[b], 16)

                def scatter(s, b, k):
                    pool.wait_ge(l.y_sb, s + 1)
                    wait(pool, l.scattered[b], 32 * k)
                    st.hold()
                    st.done(nc.gpsimd.tensor_copy(sslot[:, b, :], sidx[:, bass.ds(s * 2, 2)]))
                    st.hold()
                    for u in range(2):
                        pool.indirect_dma_start(y_dram[n], bass.IndirectOffsetOnAxis(ap=sslot[:, b, u:u + 1], axis=0),
                                                ysb[:, b, u, :], None, bounds_check=T * TOPK - 1,
                                                oob_is_err=False).then_inc(l.scattered[b], 16)

                for s in range(2):
                    gather(s, s)
                for s in range(2, 6):
                    pool.wait_ge(l.x_T, s - 1)
                    gather(s, s % 2)

                def body(it):
                    for b in range(2):
                        s = it * 2 + b
                        scatter(s, b, it)
                        pool.wait_ge(l.x_T, s + 5)
                        gather(s + 6, b)
                st.loop((NP - 6) // 2, 4, body)
                for s in range(NP - 6, NP):
                    scatter(s, s % 2, s // 2)

            experts(0)

            def first_pass(g, b):
                pool.wait_ge(xn_hi, g + 1)
                wait(pool, g_used, g)
                nc.gpsimd.tensor_tensor(xn1[1][:, :, 0:H], xn_a[:, b], xn1[0][:, :, 0:H].bitcast(F32),
                                        ALU.subtract).then_inc(xn_lo, 1)
                v = qk[:, b].rearrange("p u (h j c) -> p u h j c", j=HD // 2, c=2)
                pool.wait_ge(rot_parts, g + 1)
                r, i = v[:, :, :, 0:ROT, 0], v[:, :, :, 0:ROT, 1]
                for u in range(2):
                    nc.gpsimd.tensor_tensor(r[:, u], r[:, u], rotr[:, u], ALU.subtract)
                for u in range(2):
                    ins = nc.gpsimd.tensor_tensor(i[:, u], i[:, u], roti[:, u], ALU.add)
                ins.then_inc(rot_done, 1)
                pool.wait_ge(k_hi, g + 1)
                nc.gpsimd.tensor_tensor(aT[1].rearrange("p u c k -> p u (c k)"), qk[:, b, :, H:2 * H],
                                        aT[0].rearrange("p u c k -> p u (c k)").bitcast(F32),
                                        ALU.subtract).then_inc(k_lo, 1)

            def body(it):
                for b in range(2):
                    first_pass(it * 2 + b, b)
            repeat(pool, NG // 2, body)
            pool.wait_ge(mid_dve, 4)
            make_iotas_at = st.n
            make_iotas()
            pool.sem_inc(iotas_made, 1)
            experts(1)

        @block.scalar
        def _(act):
            def load_raw(e, b):
                act.dma_start(raw[:, b, 0:KC * F].rearrange("p (c f) -> p c f", c=KC),
                              Wup[bass.ds(e, 1)].rearrange("a (c p) f -> p (a c) f", p=P)).then_inc(raw_loaded[b], 16)
                act.dma_start(raw[:, b, KC * F:KC * (F + H)].rearrange("p (c f) -> p c f", c=KC),
                              Wdn[bass.ds(e, 1)].rearrange("a (c p) f -> p (a c) f", p=P)).then_inc(raw_loaded[b], 16)

            def load_bias():
                segs = ((bup.rearrange("e f -> (e f)"), 0, 32), (bdn.rearrange("e f -> (e f)"), 32, 16),
                        (bq, 48, 2), (bk, 50, 2), (bo, 52, 2))
                for src, at, n in segs:
                    act.dma_start(bstage[:, at:at + n], src.rearrange("(p c) -> p c", p=P)).then_inc(bias_loaded, 16)

            load_bias()
            load_raw(0, 0)
            load_raw(1, 1)
            act.wait_ge(bias_split, 1)
            for at, n, col in ((0, 32, B_UP), (32, 16, B_DN), (48, 2, B_QK), (50, 2, B_QK + H), (52, 2, B_O)):
                for k in range(3):
                    act.dma_start(bias_dram[k, col:col + P * n].rearrange("(p c) -> p c", p=P),
                                  bparts[:, k, at:at + n]).then_inc(bias_stored, 16)
            act.wait_ge(bias_stored, 16 * 15)
            act.wait_ge(bias_zeroed, 1)
            act.dma_start(biases[0:3, :], bias_dram[:, :]).then_inc(bias_ready, 16)

            def high(e, b, k):
                act.wait_ge(raw_loaded[b], 32 * (k + 1))
                nc.scalar.activation(up_w[0][:, :, bass.ds(e, 1), :].rearrange("p c a f -> p c (a f)"),
                                     raw[:, b, 0:KC * F].rearrange("p (c f) -> p c f", c=KC), ACT.Copy)
                nc.scalar.activation(dn_w[0][:, :, bass.ds(e, 1), :].rearrange("p c a f -> p c (a f)"),
                                     raw[:, b, KC * F:KC * (F + H)].rearrange("p (c f) -> p c f", c=KC),
                                     ACT.Copy).then_inc(raw_hi, 1)

            def sqrt_var(l, b, g):
                act.wait_ge(l.var, g + 1)
                nc.scalar.activation(small[:, 8 + 2 * b:10 + 2 * b], small[:, 4 + 2 * b:6 + 2 * b],
                                     ACT.Sqrt).then_inc(l.sd, 1)

            def norm_step(l, g, b, last=False, xTout=xTf):
                if not last:
                    sqrt_var(l, 1 - b, g + 1)
                act.wait_ge(l.xn_T, g + 1)
                nc.scalar.activation(xTout[:, b], ps[:, b, :].rearrange("p (u c t) -> p u c t", u=2, c=KC),
                                     ACT.Copy).then_inc(l.xn_Tsb, 1)

            sqrt_var(L[0], 0, 0)
            for e in range(2):
                high(e, e, 0)
            def body(it):
                for b in range(2):
                    norm_step(L[0], it * 2 + b, b)
            repeat(act, NG // 2 - 1, body)
            norm_step(L[0], NG - 2, 0)
            norm_step(L[0], NG - 1, 1, last=True)
            for e in range(2, E):
                act.wait_ge(raw_lo, e - 1)
                load_raw(e, e % 2)
                high(e, e % 2, e // 2)
            act.wait_ge(raw_lo, E - 1)
            for w, c in ((Wq, 0), (Wk, H)):
                act.dma_start(raw[:, 0, 0:KC * 2 * H].rearrange("p (c f) -> p c f", c=KC)[:, :, c:c + H],
                              w.rearrange("(c p) f -> p c f", p=P)).then_inc(raw_loaded[0], 16)
            act.wait_ge(raw_loaded[0], 32 * (E // 2 + 1))
            nc.scalar.activation(qk_w[0][:, :, :], raw[:, 0, 0:KC * 2 * H].rearrange("p (c f) -> p c f", c=KC),
                                 ACT.Copy).then_inc(raw_hi, 1)

            def gates(l):
                act.wait_ge(l.gap, 1)
                nc.scalar.activation(gate[:, 1, :], small[:, 16:16 + NT], ACT.Sigmoid)
                nc.scalar.activation(gate[:, 0, :], small[:, 16:16 + NT], ACT.Sigmoid, scale=-1.0).then_inc(l.gates, 1)

            def experts(l):
                def x_hi(s, b):
                    act.wait_ge(l.x_T, s + 1)
                    nc.scalar.activation(xT[0][:, b], ps[:, b, :].rearrange("p (u c t) -> p u c t", u=2, c=KC),
                                         ACT.Copy).then_inc(l.x_hi, 1)

                def a_hi(s):
                    act.wait_ge(l.a_T, s + 1)
                    nc.scalar.activation(aT[0][:, :, :, :], ps[:, 6, :].rearrange("p (u c t) -> p u c t", u=2, c=KC),
                                         ACT.Copy).then_inc(l.a_hi, 1)

                def glus(s, b):
                    wait(act, l.act, s - 1)
                    for u in range(2):
                        act.wait_ge(l.gu, s * 2 + u + 1)
                        nc.scalar.activation(glu[:, b, u, :],
                                             ps[:, 2 + 2 * b + u, :].rearrange("p (f c) -> p f c", c=2)[:, :, 0],
                                             ACT.Gelu_apprx_sigmoid).then_inc(l.glu, 1)

                def y_out(s, b, k):
                    act.wait_ge(l.y_ps, s + 1)
                    wait(act, l.scattered[b], 32 * k)
                    nc.scalar.activation(ysb[:, b], ps[:, 7, :].rearrange("p (u h) -> p u h", u=2),
                                         ACT.Copy).then_inc(l.y_sb, 1)

                x_hi(0, 0)
                x_hi(1, 1)
                glus(0, 0)
                def body(it):
                    for d in range(2):
                        s, b = it * 2 + 1 + d, (1 + d) % 2
                        x_hi(s + 1, 1 - b)
                        a_hi(s - 1)
                        glus(s, b)
                        y_out(s - 1, 1 - b, it)
                repeat(act, NP // 2 - 1, body)
                a_hi(NP - 2)
                glus(NP - 1, 1)
                y_out(NP - 2, 0, NP // 2 - 1)
                a_hi(NP - 1)
                y_out(NP - 1, 1, NP // 2 - 1)

            gates(L[0])
            experts(L[0])

            def xT_high(g, b):
                act.wait_ge(A.x_T, g + 1)
                nc.scalar.activation(xT[0][:, b], ps[:, b, :].rearrange("p (u c t) -> p u c t", u=2, c=KC),
                                     ACT.Copy).then_inc(A.x_hi, 1)

            def xn_high(g, b):
                act.wait_ge(A.xn, g + 1)
                wait(act, g_used, g)
                nc.scalar.activation(xn1[0][:, :, 0:H], xn_a[:, b], ACT.Copy).then_inc(xn_hi, 1)

            def qk_out(g, b, k):
                act.wait_ge(qk_ps, g + 1)
                wait(act, q_stored[b], 16 * k)
                wait(act, k_lo, g - 1)
                nc.scalar.activation(qk[:, b], ps[:, 2 + 2 * b:4 + 2 * b, :], ACT.Copy).then_inc(qk_sb, 1)

            def k_high(g, b):
                act.wait_ge(rot_done, g + 1)
                wait(act, g_used, g)
                nc.scalar.activation(aT[0].rearrange("p u c k -> p u (c k)"), qk[:, b, :, H:2 * H],
                                     ACT.Copy).then_inc(k_hi, 1)

            def first_pass(g, b, k, last=False):
                if not last:
                    sqrt_var(A, 1 - b, g + 1)
                xT_high(g, b)
                qk_out(g - 1, 1 - b, k - 1 + b)
                k_high(g - 1, 1 - b)
                xn_high(g, b)

            sqrt_var(A, 0, 0)
            sqrt_var(A, 1, 1)
            xT_high(0, 0)
            xn_high(0, 0)
            first_pass(1, 1, 0)
            first_pass(2, 0, 1)
            def body(it):
                for d in range(2):
                    g, b = it * 2 + 3 + d, (3 + d) % 2
                    first_pass(g, b, it + 1 + d)
            repeat(act, NG // 2 - 2, body)
            first_pass(NG - 1, 1, NG // 2 - 1, last=True)
            qk_out(NG - 1, 1, NG // 2 - 1)
            k_high(NG - 1, 1)

            act.wait_ge(mid_pe, 4)
            nc.scalar.activation(qk_w[0][:, :, 0:H], ps[:, 4, :].rearrange("p (a o) -> p a o", a=KC),
                                 ACT.Copy).then_inc(m_hi, 1)

            def q_high(g, b):
                act.wait_ge(q_T, g + 1)
                nc.scalar.activation(xT[0][:, b], ps[:, 2 + b, :].rearrange("p (u c t) -> p u c t", u=2, c=KC),
                                     ACT.Copy).then_inc(q_hi, 1)

            q_high(0, 0)
            q_high(1, 1)
            sqrt_var(L[1], 0, 0)
            def body(it):
                for b in range(2):
                    g = it * 2 + b
                    q_high(g + 2, b)
                    norm_step(L[1], g, b)
            repeat(act, NG // 2 - 1, body)
            norm_step(L[1], NG - 2, 0)
            norm_step(L[1], NG - 1, 1, last=True)
            gates(L[1])
            experts(L[1])

        @block.tensor
        def _(pe):
            def transpose4(bank, src):
                for u in range(2):
                    for c in range(KC):
                        k = (u * KC + c) * P
                        ins = nc.tensor.transpose(ps[:, bank, k:k + P], src[:, u, c * P:(c + 1) * P], ident)
                return ins

            def bias(out, at, width, start=True):
                nc.tensor.matmul(out, ones[:, :], biases[:, bass.ds(at, width)], start=True, stop=False)

            def product(out, st_hi, st_lo, mv_hi, mv_lo, stop):
                nc.tensor.matmul(out, st_hi, mv_hi, start=False, stop=False)
                nc.tensor.matmul(out, st_hi, mv_lo, start=False, stop=False)
                return nc.tensor.matmul(out, st_lo, mv_hi, start=False, stop=stop)

            pe.wait_ge(consts_loaded, 16)
            pe.wait_ge(consts_made, 1)
            pe.wait_ge(small_loaded, 64)

            def xn_transpose(l, src, g, b, bank_free):
                pe.wait_ge(l.xn, g + 1)
                wait(pe, bank_free, g - 1)
                transpose4(b, src[:, b]).then_inc(l.xn_T, 1)

            def logits(l, g, b):
                pe.wait_ge(l.xn_Tsb, g + 1)
                for u in range(2):
                    for c in range(KC):
                        ins = nc.tensor.matmul(ps[:, 7, bass.ds(g * 2 * E + u * E, E)], xTf[:, b, u, c, :],
                                               wr[:, c, :], start=(c == 0), stop=(c == KC - 1))
                ins.then_inc(l.logits, 1)

            def layer_norm_loop(l):
                xn_transpose(l, xn_r, 0, 0, l.xn_Tsb)
                def body(it):
                    for b in range(2):
                        g = it * 2 + b
                        xn_transpose(l, xn_r, g + 1, 1 - b, l.xn_Tsb)
                        logits(l, g, b)
                repeat(pe, NG // 2 - 1, body)
                xn_transpose(l, xn_r, NG - 1, 1, l.xn_Tsb)
                logits(l, NG - 2, 0)
                logits(l, NG - 1, 1)

            def route(l):
                pe.wait_ge(l.mask, 1)
                m = area(0, 256, dt=BF16)
                nc.tensor.matmul(ps[:, 2, 0:NT * E], upper[:, :], m, start=True, stop=True)
                nc.tensor.matmul(ps[:, 2, NT * E:2 * NT * E], ones[:, :], m, start=True, stop=True).then_inc(l.prefix, 1)
                for c in range(NQC):
                    pe.wait_ge(l.hot, c + 1)
                    hs, hc, hp = hot(c % 2)
                    for k in range(QC):
                        first, last = c == 0 and k == 0, c == NQC - 1 and k == QC - 1
                        nc.tensor.matmul(ps[:, 3, 0:NS], hs[:, :, k], hc[:, :, k], start=first, stop=last)
                        ins = nc.tensor.matmul(ps[:, 4, 0:NS], hs[:, :, k], hp[:, :, k], start=first, stop=last)
                    ins.then_inc(l.hot_used, 1)

            def experts(l):
                pe.wait_ge(l.routed, 1)
                pe.wait_ge(raw_lo, E + 1)
                pe.wait_ge(raw_hi, E + 1)
                pe.wait_ge(bias_ready, 16)

                def name(j):
                    return pe.value_load(expert[0:1, bass.ds(j, 1)], min_val=0, max_val=E - 1)

                def x_transpose(s, b, k):
                    pe.wait_ge(l.gathered[b], 32 * (k + 1))
                    wait(pe, l.x_lo, s - 1)
                    transpose4(b, xg[:, b]).then_inc(l.x_T, 1)

                def up(s, b, u):
                    e = name(s * 2 + u)
                    if u == 0:
                        pe.wait_ge(l.x_hi, s + 1)
                        pe.wait_ge(l.x_lo, s + 1)
                        wait(pe, l.act, s - 1)
                    o = ps[:, 2 + 2 * b + u, :]
                    bias(o, e * F + B_UP, F)
                    for c in range(KC):
                        ins = product(o, xT[0][:, b, u, c, :], xT[1][:, b, u, c, :],
                                      up_w[0][:, c, bass.ds(e, 1), :], up_w[1][:, c, bass.ds(e, 1), :], c == KC - 1)
                    ins.then_inc(l.gu, 1)

                def a_transpose(s, b):
                    pe.wait_ge(l.act, s + 1)
                    wait(pe, l.a_lo, s)
                    transpose4(6, act_v[:, b]).then_inc(l.a_T, 1)

                def down(s):
                    e = [name(s * 2 + u) for u in range(2)]
                    pe.wait_ge(l.a_hi, s + 1)
                    pe.wait_ge(l.a_lo, s + 1)
                    wait(pe, l.y_sb, s)
                    for u in range(2):
                        o = ps[:, 7, u * H:(u + 1) * H]
                        bias(o, e[u] * H + B_DN, H)
                        for c in range(KC):
                            ins = product(o, aT[0][:, u, c, :], aT[1][:, u, c, :],
                                          dn_w[0][:, c, bass.ds(e[u], 1), :], dn_w[1][:, c, bass.ds(e[u], 1), :],
                                          c == KC - 1)
                    ins.then_inc(l.y_ps, 1)

                x_transpose(0, 0, 0)
                x_transpose(1, 1, 0)
                up(0, 0, 0)
                up(0, 0, 1)
                def body(it):
                    for d in range(2):
                        s, b = it * 2 + 1 + d, (1 + d) % 2
                        x_transpose(s + 1, 1 - b, it + 1)
                        up(s, b, 0)
                        a_transpose(s - 1, 1 - b)
                        up(s, b, 1)
                        down(s - 1)
                repeat(pe, NP // 2 - 1, body)
                up(NP - 1, 1, 0)
                a_transpose(NP - 2, 0)
                up(NP - 1, 1, 1)
                down(NP - 2)
                a_transpose(NP - 1, 1)
                down(NP - 1)

            layer_norm_loop(L[0])
            route(L[0])
            experts(L[0])

            def a_in(g, b):
                pe.wait_ge(A.xn, g + 1)
                wait(pe, A.x_lo, g - 1)
                transpose4(b, xn_a[:, b]).then_inc(A.x_T, 1)

            def project(g, b):
                pe.wait_ge(A.x_hi, g + 1)
                pe.wait_ge(A.x_lo, g + 1)
                wait(pe, qk_sb, g - 1)
                for u in range(2):
                    o = ps[:, 2 + 2 * b + u, :]
                    bias(o, B_QK, 2 * H)
                    for c in range(KC):
                        ins = product(o, xT[0][:, b, u, c, :], xT[1][:, b, u, c, :], qk_w[0][:, c, :], qk_w[1][:, c, :],
                                      c == KC - 1)
                ins.then_inc(qk_ps, 1)

            def key_sums(g, first=False, last=False):
                pe.wait_ge(k_hi, g + 1)
                pe.wait_ge(k_lo, g + 1)
                pe.wait_ge(xn_lo, g + 1)
                for u in range(2):
                    for a in range(KC):
                        o = ps[:, 6 + a, 0:H + 2]
                        hi, lo = aT[0][:, u, a, :], aT[1][:, u, a, :]
                        nc.tensor.matmul(o, hi, xn1[0][:, u, :], start=first and u == 0, stop=False, skip_group_check=True)
                        nc.tensor.matmul(o, hi, xn1[1][:, u, :], start=False, stop=False, skip_group_check=True)
                        ins = nc.tensor.matmul(o, lo, xn1[0][:, u, :], start=False, stop=last and u == 1,
                                               skip_group_check=True)
                ins.then_inc(g_used, 1)

            a_in(0, 0)
            a_in(1, 1)
            project(0, 0)
            project(1, 1)
            key_sums(0, first=True)
            def body(it):
                for b in range(2):
                    g = it * 2 + b + 2
                    a_in(g, b)
                    project(g, b)
                    key_sums(g - 1)
            repeat(pe, NG // 2 - 1, body)
            key_sums(NG - 1, last=True)

            pe.wait_ge(mid_dve, 1)
            for c in range(KC):
                for a in range(KC):
                    nc.tensor.transpose(ps[:, 2, (c * KC + a) * P:(c * KC + a + 1) * P],
                                        gsb[:, a, c * P:(c + 1) * P], ident)
            for a in range(KC):
                ins = nc.tensor.transpose(ps[0:2, 3, a * P:(a + 1) * P], gsb[:, a, H:H + 2], ident)
            ins.then_inc(mid_pe, 1)
            pe.wait_ge(mid_dve, 2)
            for a in range(KC):
                o = ps[:, 5, a * P:(a + 1) * P]
                for c in range(KC):
                    nc.tensor.matmul(o, wv[:, c, a * P:(a + 1) * P], gT[:, c, a * P:(a + 1) * P],
                                     start=(c == 0), stop=False)
                ins = nc.tensor.matmul(o, bvrow[0:1, a * P:(a + 1) * P], ksT[0:1, a * P:(a + 1) * P],
                                       start=False, stop=True)
            ins.then_inc(mid_pe, 2)
            pe.wait_ge(mid_dve, 3)
            for a in range(KC):
                ins = nc.tensor.matmul(ps[:, 4, a * H:(a + 1) * H], sT[:, a, :], wo[:, a, :], start=True, stop=True)
            ins.then_inc(mid_pe, 1)

            def q_transpose(g, b, k):
                pe.wait_ge(q_loaded[b], 16 * (k + 1))
                wait(pe, q_lo, g - 1)
                transpose4(2 + b, qin[:, b]).then_inc(q_T, 1)

            def attend(g, b):
                pe.wait_ge(q_hi, g + 1)
                pe.wait_ge(q_lo, g + 1)
                wait(pe, x_done, g - 1)
                for u in range(2):
                    o = ps[:, 4 + b, u * H:(u + 1) * H]
                    bias(o, B_O, H)
                    for a in range(KC):
                        ins = product(o, xT[0][:, b, u, a, :], xT[1][:, b, u, a, :], qk_w[0][:, a, 0:H],
                                      qk_w[1][:, a, 0:H], a == KC - 1)
                ins.then_inc(o_ps, 1)

            pe.wait_ge(mid_dve, 4)
            q_transpose(0, 0, 0)
            q_transpose(1, 1, 0)
            pe.wait_ge(m_hi, 1)
            pe.wait_ge(m_lo, 1)
            attend(0, 0)
            l = L[1]

            def norm_in(g, b):
                pe.wait_ge(l.xn, g + 1)
                wait(pe, l.xn_Tsb, g - 1)
                transpose4(b, xn_r[:, b]).then_inc(l.xn_T, 1)

            def body(it):
                for b in range(2):
                    g = it * 2 + b
                    attend(g + 1, 1 - b)
                    q_transpose(g + 2, b, it + 1)
                    norm_in(g, b)
                    logits(l, g, b)
            repeat(pe, NG // 2 - 1, body)
            attend(NG - 1, 1)
            norm_in(NG - 2, 0)
            logits(l, NG - 2, 0)
            norm_in(NG - 1, 1)
            logits(l, NG - 1, 1)
            route(l)
            experts(l)

        @block.vector
        def _(dve):
            v = nc.vector
            st = Steps(dve, dve_step, dve_passed)
            dve.wait_ge(consts_loaded, 16)
            v.memset(ones[:, :], 1.0)
            v.tensor_copy(upper[:, :], cst[:, C_UP:C_UP + P]).then_inc(consts_made, 1)
            v.memset(xn1[0][:, :, H:H + 1].bitcast(F32), 1.0)
            v.memset(xn1[0][:, :, H + 1:H + 2].bitcast(F32), 0.0)
            v.memset(xn1[1][:, :, H:H + 2].bitcast(F32), 0.0)

            dve.wait_ge(bias_loaded, 80)
            odd = bstage[:, 0:32].rearrange("p (f c) -> p f c", c=2)[:, :, 1]
            st.done(v.tensor_scalar(odd, odd, 1.0, None, ALU.add))
            st.done(v.tensor_copy(bparts[:, 0, :], bstage[:, :]))
            st.done(v.tensor_tensor(bres[:, :], bstage[:, :], bparts[:, 0, :], ALU.subtract))
            st.done(v.tensor_copy(bparts[:, 1, :], bres[:, :]))
            st.done(v.tensor_tensor(bres[:, :], bres[:, :], bparts[:, 1, :], ALU.subtract))
            v.tensor_copy(bparts[:, 2, :], bres[:, :]).then_inc(bias_split, 1)

            mv = [[sbmv[:, 4 * b + 2 * u:4 * b + 2 * u + 2] for u in range(2)] for b in range(2)]

            def moments(l, g, b):
                st.hold()
                for u in range(2):
                    ins = v.bn_stats(bst[:, u, :], xs[:, bass.ds(g * 2 + u, 1), :].rearrange("p a h -> p (a h)"))
                st.done(ins)
                st.hold()
                for u in range(2):
                    ins = v.bn_aggr(mv[b][u], bst[:, u, :])
                st.done(ins)
                v.tensor_scalar(small[:, 4 + 2 * b:6 + 2 * b],
                                sbmv[:, 4 * b:4 * b + 4].rearrange("p (u c) -> p u c", c=2)[:, :, 1],
                                EPS, None, ALU.add).then_inc(l.var, 1)

            def normalise(l, dst, g, b):
                dve.wait_ge(l.sd, g + 1)
                st.done(v.reciprocal(small[:, 12 + 2 * b:14 + 2 * b], small[:, 8 + 2 * b:10 + 2 * b]))
                for u in range(2):
                    ins = v.tensor_scalar(dst[:, b, u, :], xs[:, bass.ds(g * 2 + u, 1), :].rearrange("p a h -> p (a h)"),
                                          mv[b][u][:, 0:1], small[:, 12 + 2 * b + u:13 + 2 * b + u],
                                          ALU.subtract, ALU.mult)
                ins.then_inc(l.xn, 1)

            l = L[0]
            dve.wait_ge(x_loaded[0], 16)
            moments(l, 0, 0)
            for c in range(1, 4):
                dve.wait_ge(x_loaded[c], 16)

            def ln_step(g, b, k, last=False):
                if not last:
                    moments(l, g + 1, 1 - b)
                wait(dve, l.xn_stored[b], 16 * k)
                wait(dve, l.xn_T, g - 1)
                normalise(l, xn_r, g, b)

            def ln_body(it):
                for b in range(2):
                    ln_step(it * 2 + b, b, it)
            st.loop(NG // 2 - 1, 6, ln_body)
            ln_step(NG - 2, 0, NG // 2 - 1)
            ln_step(NG - 1, 1, NG // 2 - 1, last=True)

            def route(n):
                l = L[n]
                mask = area(0, NT * E, dt=BF16)
                lg = area(256, NT, E)
                eq = area(512, NT, E)
                cand = area(768, NT, E)
                oh = [area(1024 + 256 * k, NT, E) for k in range(2)]
                prod = area(1536, NT, E)
                scan = [area(6208 + 400 * k, PAD + NT, E) for k in range(2)]
                top = area(7040, 2, NT)
                pick = area(7104, NT)
                pos = area(7136, NT, TOPK)
                posi = area(7200, 2, NQ, dt=I32)
                posb = area(7328, 2, NQ, dt=BF16)
                tiles = area(7400, 2, 16)
                tilei = area(7440, 16, dt=I32)
                nam = area(7460, 2, NS)
                cmp = area(512, NS, E)
                dve.wait_ge(l.logits, NG)
                dve.wait_ge(iotas_made, n + 1)
                if n == 0:
                    dve.wait_ge(raw_lo, E + 1)
                    dve.wait_ge(bias_ready, 16)
                for b in range(2):
                    dve.wait_ge(l.xn_stored[b], 16 * (NG // 2))
                st.done(v.tensor_copy(lg, ps[:, 7, 0:NT * E].rearrange("p (i e) -> p i e", e=E)))
                eiota = cst[:, None, C_E:C_E + E].to_broadcast([P, NT, E])
                for k in range(TOPK):
                    st.done(v.tensor_reduce(top[:, k, :], lg, AX.X, ALU.max))
                    st.done(v.tensor_tensor(eq, lg, top[:, k, :, None].to_broadcast([P, NT, E]), ALU.is_equal))
                    st.done(v.scalar_tensor_tensor(out=cand, in0=eq, scalar=-float(E), in1=eiota,
                                                   op0=ALU.mult, op1=ALU.add))
                    st.done(v.tensor_reduce(pick, cand, AX.X, ALU.min))
                    st.done(v.tensor_tensor(oh[k], cand, pick[:, :, None].to_broadcast([P, NT, E]), ALU.is_equal))
                    if k == 0:
                        st.done(v.scalar_tensor_tensor(out=lg, in0=oh[0], scalar=MASKED, in1=lg,
                                                       op0=ALU.mult, op1=ALU.add))
                v.tensor_tensor(small[:, 16:16 + NT], top[:, 1, :], top[:, 0, :], ALU.subtract).then_inc(l.gap, 1)
                v.tensor_tensor(mask.rearrange("p (i e) -> p i e", e=E), oh[0], oh[1], ALU.add).then_inc(l.mask, 1)
                for k in range(2):
                    st.done(v.memset(scan[k][:, 0:PAD, :], 0.0))
                v.memset(tiles[:, :, 0:8], 0.0)
                dve.wait_ge(l.prefix, 1)
                st.done(v.tensor_copy(scan[0][:, PAD:, :],
                                      ps[:, 2, NT * E:2 * NT * E].rearrange("p (i e) -> p i e", e=E)))
                a = 0
                for d in (1, 2, 4, 8, 16):
                    st.done(v.tensor_tensor(scan[1 - a][:, PAD:, :], scan[a][:, PAD:, :],
                                            scan[a][:, PAD - d:PAD + NT - d, :], ALU.add))
                    a = 1 - a
                st.done(v.tensor_scalar(tilei[:, 0:E], scan[a][:, PAD + NT - 1, :], float(P - 1), None, ALU.add))
                st.done(v.tensor_single_scalar(tilei[:, 0:E], tilei[:, 0:E], 7, ALU.logical_shift_right))
                st.done(v.tensor_copy(tiles[:, 0, 8:16], tilei[:, 0:E]))
                c = 0
                for d in (1, 2, 4):
                    st.done(v.tensor_tensor(tiles[:, 1 - c, 8:16], tiles[:, c, 8:16], tiles[:, c, 8 - d:16 - d],
                                            ALU.add))
                    c = 1 - c
                before = tiles[:, c, 7:15]
                st.done(v.tensor_tensor(prod, ps[:, 2, 0:NT * E].rearrange("p (i e) -> p i e", e=E),
                                        scan[a][:, PAD - 1:PAD + NT - 1, :], ALU.add))
                st.done(v.scalar_tensor_tensor(out=prod, in0=before[:, None, :].to_broadcast([P, NT, E]), scalar=float(P),
                                               in1=prod, op0=ALU.mult, op1=ALU.add))
                for k in range(TOPK):
                    st.done(v.tensor_tensor(oh[k], oh[k], prod, ALU.mult))
                    st.done(v.tensor_reduce(pos[:, :, k], oh[k], AX.X, ALU.add))
                st.done(v.tensor_copy(posi[:, 1, :], pos.rearrange("p i k -> p (i k)")))
                st.done(v.tensor_single_scalar(posi[:, 0, :], posi[:, 1, :], 7, ALU.logical_shift_right))
                st.done(v.tensor_single_scalar(posi[:, 1, :], posi[:, 1, :], P - 1, ALU.bitwise_and))
                st.done(v.tensor_copy(posb, posi))
                row = slice(0, 1)
                st.done(v.tensor_tensor(cmp[row, :, 1:E], before[row, None, 1:E].to_broadcast([1, NS, E - 1]),
                                        iotaJ[row, :, 0:1].to_broadcast([1, NS, E - 1]), ALU.is_le))
                st.done(v.tensor_reduce(nam[row, 0, :], cmp[row, :, 1:E], AX.X, ALU.add))
                st.done(v.tensor_copy(expert[:, :], nam[row, 0, :]))
                for ch in range(NQC):
                    if ch >= 2:
                        dve.wait_ge(l.hot_used, ch - 1)
                    hs, hc, hp = hot(ch % 2)
                    cols = slice(ch * QC, (ch + 1) * QC)
                    st.done(v.tensor_tensor(hp, iotaJ, posb[:, 0, None, cols].to_broadcast([P, NS, QC]), ALU.is_equal))
                    v.tensor_tensor(hs, iotaS, posb[:, 1, None, cols].to_broadcast([P, P, QC]), ALU.is_equal)
                    st.done(v.scalar_tensor_tensor(out=hc, in0=qnum, scalar=float(ch * QC), in1=hp,
                                                   op0=ALU.add, op1=ALU.mult))
                    v.tensor_scalar(hp, hp, cst[:, C_P:C_P + 1], None, ALU.mult).then_inc(l.hot, 1)
                dve.wait_ge(l.hot_used, NQC)
                st.done(v.tensor_copy(nam[:, 1, :], ps[:, 3, 0:NS]))
                st.done(v.scalar_tensor_tensor(out=nam[:, 1, :], in0=ps[:, 4, 0:NS], scalar=float(NQ),
                                               in1=nam[:, 1, :], op0=ALU.mult, op1=ALU.add))
                st.done(v.tensor_scalar(nam[:, 0, :], nam[:, 1, :], 0.0, SKIP, ALU.is_equal, ALU.mult))
                v.scalar_tensor_tensor(out=sidx[:, :], in0=nam[:, 1, :], scalar=-1.0, in1=nam[:, 0, :],
                                       op0=ALU.add, op1=ALU.add)
                st.done(v.tensor_scalar(gidx[:, :], nam[:, 1, :], -1.0, 0.0, ALU.add, ALU.max))
                st.done(v.tensor_single_scalar(gidx[:, :], gidx[:, :], 1, ALU.logical_shift_right))
                dve.wait_ge(l.gates, 1)
                st.done(v.tensor_scalar(gate[:, :, :], gate[:, :, :], 0.5, None, ALU.mult))
                v.engine_nop().then_inc(l.routed, 1)

            def experts(l):
                def x_lo(s, b):
                    dve.wait_ge(l.x_hi, s + 1)
                    v.tensor_tensor(xT[1][:, b], ps[:, b, :].rearrange("p (u c t) -> p u c t", u=2, c=KC),
                                    xT[0][:, b].bitcast(F32), ALU.subtract).then_inc(l.x_lo, 1)

                def a_lo(s):
                    dve.wait_ge(l.a_hi, s + 1)
                    v.tensor_tensor(aT[1][:, :, :, :], ps[:, 6, :].rearrange("p (u c t) -> p u c t", u=2, c=KC),
                                    aT[0][:, :, :, :].bitcast(F32), ALU.subtract).then_inc(l.a_lo, 1)

                def activate(s, b):
                    for u in range(2):
                        dve.wait_ge(l.glu, s * 2 + u + 1)
                        ins = v.tensor_scalar(upv[:, u, :],
                                              ps[:, 2 + 2 * b + u, :].rearrange("p (f c) -> p f c", c=2)[:, :, 1],
                                              1.0 - LIMIT, 1.0 + LIMIT, ALU.max, ALU.min)
                    st.done(ins)
                    v.scalar_tensor_tensor(out=act_v[:, b], in0=glu[:, b], scalar=GLU_LIMIT, in1=upv[:, :, :],
                                           op0=ALU.min, op1=ALU.mult).then_inc(l.act, 1)

                x_lo(0, 0)
                x_lo(1, 1)
                activate(0, 0)

                def body(it):
                    for d in range(2):
                        s, b = it * 2 + 1 + d, (1 + d) % 2
                        x_lo(s + 1, 1 - b)
                        a_lo(s - 1)
                        activate(s, b)
                st.loop(NP // 2 - 1, 2, body)
                a_lo(NP - 2)
                activate(NP - 1, 1)
                a_lo(NP - 1)

            def combine(l, g, b, k):
                dve.wait_ge(l.y_loaded[b], 16 * (k + 1))
                for c in range(TOPK):
                    for u in range(2):
                        xr = xs[:, bass.ds(g * 2 + u, 1), :].rearrange("p a h -> p (a h)")
                        ins = v.scalar_tensor_tensor(out=xr, in0=ybuf[:, b, u, c, :],
                                                     scalar=gate[:, c, bass.ds(g * 2 + u, 1)], in1=xr,
                                                     op0=ALU.mult, op1=ALU.add)
                    if c == 0:
                        st.done(ins)
                ins.then_inc(l.y_used, 1)
                dve.wait_ge(l.y_used, g + 1)

            route(0)
            experts(L[0])

            def xT_low(g, b):
                dve.wait_ge(A.x_hi, g + 1)
                v.tensor_tensor(xT[1][:, b], ps[:, b, :].rearrange("p (u c t) -> p u c t", u=2, c=KC),
                                xT[0][:, b].bitcast(F32), ALU.subtract).then_inc(A.x_lo, 1)

            def rotate(g, b):
                dve.wait_ge(qk_sb, g + 1)
                wait(dve, rot_done, g)
                for u in range(2):
                    w = qk[:, b, u, :].rearrange("p (h j c) -> p h j c", j=HD // 2, c=2)
                    sin = cst[:, bass.ds(g * 2 * ROT + (C_SIN + u * ROT), ROT)][:, None, :].to_broadcast(
                        [P, 2 * HEADS, ROT])
                    v.tensor_tensor(rotr[:, u], w[:, :, 0:ROT, 1], sin, ALU.mult)
                    ins = v.tensor_tensor(roti[:, u], w[:, :, 0:ROT, 0], sin, ALU.mult)
                st.done(ins)
                for u in range(2):
                    w = qk[:, b, u, :].rearrange("p (h j c) -> p h j c", j=HD // 2, c=2)
                    ins = v.tensor_scalar(w[:, :, 0, :], w[:, :, 0, :], cst[:, bass.ds(g * 2 + (C_COS + u), 1)], None,
                                          ALU.mult)
                ins.then_inc(rot_parts, 1)

            def attn_step(g, b, k, last=False):
                if not last:
                    combine(L[0], g + 1, 1 - b, k + b)
                    moments(A, g + 1, 1 - b)
                wait(dve, A.x_T, g - 1)
                wait(dve, xn_lo, g - 1)
                normalise(A, xn_a, g, b)
                xT_low(g, b)

            combine(L[0], 0, 0, 0)
            moments(A, 0, 0)
            attn_step(0, 0, 0)
            attn_step(1, 1, 0)

            def attn_body(it):
                for b in range(2):
                    g = it * 2 + b + 2
                    rotate(g - 2, b)
                    attn_step(g, b, it + 1)
            st.loop(NG // 2 - 2, 10, attn_body)
            rotate(NG - 4, 0)
            attn_step(NG - 2, 0, NG // 2 - 1)
            rotate(NG - 3, 1)
            attn_step(NG - 1, 1, NG // 2 - 1, last=True)
            rotate(NG - 2, 0)
            rotate(NG - 1, 1)

            dve.wait_ge(g_used, NG)
            dve.wait_ge(q_stored[0], 16 * (NG // 2))
            v.tensor_copy(gsb, ps[:, 6:8, 0:H + 2]).then_inc(mid_dve, 1)
            dve.wait_ge(mid_pe, 1)
            v.tensor_copy(gT.rearrange("p c o -> p (c o)"), ps[:, 2, :])
            v.tensor_copy(ksT[0:1, :], ps[0:1, 3, 0:H]).then_inc(mid_dve, 1)
            dve.wait_ge(mid_pe, 3)
            v.tensor_tensor(sT, ps[:, 5, 0:KC * P].rearrange("p (a k) -> p a k", a=KC),
                            cst[:, None, C_BLK:C_BLK + P].to_broadcast([P, KC, P]), ALU.mult).then_inc(mid_dve, 1)
            dve.wait_ge(m_hi, 1)
            v.tensor_tensor(qk_w[1][:, :, 0:H], ps[:, 4, :].rearrange("p (a o) -> p a o", a=KC),
                            qk_w[0][:, :, 0:H].bitcast(F32), ALU.subtract).then_inc(m_lo, 1)
            dve.wait_ge(m_lo, 1)
            v.engine_nop().then_inc(mid_dve, 1)

            l1 = L[1]

            def q_low(g, b):
                dve.wait_ge(q_hi, g + 1)
                v.tensor_tensor(xT[1][:, b], ps[:, 2 + b, :].rearrange("p (u c t) -> p u c t", u=2, c=KC),
                                xT[0][:, b].bitcast(F32), ALU.subtract).then_inc(q_lo, 1)

            def add_out(g, b):
                dve.wait_ge(o_ps, g + 1)
                xr = pair(xs, g)
                v.tensor_tensor(xr, xr, ps[:, 4 + b, :].rearrange("p (u h) -> p u h", u=2), ALU.add).then_inc(x_done, 1)
                dve.wait_ge(x_done, g + 1)
                moments(l1, g, b)

            def second_step(g, b, k, q=True, last=False):
                if not last:
                    add_out(g + 1, 1 - b)
                if q:
                    q_low(g + 2, b)
                dve.wait_ge(l1.xn_stored[b], 16 * k)
                dve.wait_ge(l1.xn_T, 2 * k + b - 1 if b else 2 * k)
                normalise(l1, xn_r, g, b)

            q_low(0, 0)
            q_low(1, 1)
            add_out(0, 0)

            def second_body(it):
                for b in range(2):
                    second_step(it * 2 + b, b, it)
            st.loop(NG // 2 - 1, 6, second_body)
            second_step(NG - 2, 0, NG // 2 - 1, q=False)
            second_step(NG - 1, 1, NG // 2 - 1, q=False, last=True)
            route(1)
            experts(l1)

            def last_body(it):
                for b in range(2):
                    combine(l1, it * 2 + b, b, it)
            st.loop(NG // 2, 2, last_body)


_INS = ["L0_attn_x", "L0_attn_Wq", "L0_attn_bq", "L0_attn_Wk", "L0_attn_bk", "L0_attn_Wv", "L0_attn_bv",
        "L0_attn_Wo", "L0_attn_bo", "L0_ffn_router_weight", "L0_ffn_gate_up_proj", "L0_ffn_gate_up_proj_bias",
        "L0_ffn_down_proj", "L0_ffn_down_proj_bias"]


def constants():
    import numpy as np
    c = np.zeros((P, NCONST), np.float32)
    c[:, C_ID:C_ID + P] = np.eye(P)
    c[:, C_UP:C_UP + P] = np.triu(np.ones((P, P)), 1)
    c[:, C_BLK:C_BLK + P] = np.kron(np.eye(P // HD), np.ones((HD, HD))) / np.sqrt(HD)
    freqs = np.zeros(ROT, np.float32)
    for j in range(ROT):
        freqs[j] = np.float32(1.0) / np.float32(10000.0 ** (2 * j))
    angles = np.arange(T, dtype=np.float32)[:, None] * freqs[None, :]
    c[:, C_COS:C_COS + NT] = np.cos(angles[:, 0]).reshape(P, NT)
    c[:, C_SIN:C_SIN + NT * ROT] = np.sin(angles).reshape(P, NT * ROT)
    c[:, C_P] = np.arange(P)
    c[:, C_E:C_E + E] = np.arange(E)
    return c


def kernel(**inputs):
    import numpy as np
    import concourse.bacc as bacc
    from concourse.bass_utils import run_bass_kernel_spmd

    nc = bacc.Bacc("TRN2", target_bir_lowering=False, num_devices=1)
    arrays = {name: np.ascontiguousarray(inputs[name]) for name in _INS}
    arrays["constants"] = constants()
    args = [nc.dram_tensor(name, a.shape, mybir.dt.from_np(a.dtype), kind="ExternalInput").ap()
            for name, a in arrays.items()]
    out = nc.dram_tensor("out", (1, T, H), F32, kind="ExternalOutput").ap()
    build(nc, *args, out)
    r = run_bass_kernel_spmd(nc, [arrays], core_ids=[0])
    return r.results[0]["out"]
```

```python
from contextlib import ExitStack

import concourse.bass as bass
from concourse import mybir

ALU = mybir.AluOpType
ACT = mybir.ActivationFunctionType
AX = mybir.AxisListType
F32 = mybir.dt.float32
F32R = mybir.dt.float32r
BF16 = mybir.dt.bfloat16
I32 = mybir.dt.int32
U32 = mybir.dt.uint32

P = 128
T, H = 4096, 256
NT = T // P
NG = NT // 2
KC = H // P
E, I = 8, 256
F = 2 * I
TOPK = 2
HEADS, HD = 16, 16
ROT = 5
NQ = TOPK * NT
NS = T * TOPK // P + E
NP = NS // 2
QC = 8
NQC = NQ // QC
PAD = 16
LIMIT, ALPHA = 7.0, 1.702
EPS = 1e-5
GLU_LIMIT = 6.9999536
MASKED = -3.0e38
SKIP = 16384.0

C_ID, C_UP, C_BLK = 0, P, 2 * P
C_COS = 3 * P
C_SIN = C_COS + NT
C_P = C_SIN + NT * ROT
C_E = C_P + 1
NCONST = C_E + E

B_UP, B_DN = 0, E * F
B_QK = B_DN + E * H
B_O = B_QK + 2 * H
NB = B_O + H

WORK = 9216


def wait(eng, sem, n):
    if not (isinstance(n, int) and n <= 0):
        eng.wait_ge(sem, n)


def repeat(eng, count, body):
    body(0)
    with eng.Fori(1, count) as it:
        body(it)


def stages(eng, step):
    for g in range(4):
        step(g, g, 0)
    with eng.Fori(1, NG // 4 - 1) as it:
        for j in range(4):
            step(it * 4 + j, j, it)
    for g in range(NG - 4, NG):
        step(g, g % 4, g // 4)


class Steps:

    def __init__(self, eng, sem, passed):
        self.eng, self.sem, self.passed, self.n, self.done_in_body = eng, sem, passed, 0, 0

    def hold(self):
        self.eng.sem_inc(self.passed, 1)

    def done(self, ins):
        self.n = self.n + 1
        self.done_in_body += 1
        ins.then_inc(self.sem, 1)
        self.eng.wait_ge(self.sem, self.n)

    def stages(self, per, step):
        for g in range(4):
            step(g, g, 0)
        base = self.n
        with self.eng.Fori(1, NG // 4 - 1) as it:
            self.n, self.done_in_body = base + (it - 1) * per, 0
            for j in range(4):
                step(it * 4 + j, j, it)
            assert self.done_in_body == per, self.done_in_body
        self.n = base + (NG // 4 - 2) * per
        for g in range(NG - 4, NG):
            step(g, g % 4, g // 4)

    def loop(self, count, per, body):
        base = self.n
        body(0)
        with self.eng.Fori(1, count) as it:
            self.n, self.done_in_body = base + it * per, 0
            body(it)
            assert self.done_in_body == per, self.done_in_body
        self.n = base + count * per


def build(nc, x, Wq, bq, Wk, bk, Wv, bv, Wo, bo, Wr, Wup, bup, Wdn, bdn, consts, out):
    ctx = ExitStack()

    def sb(name, shape, dt):
        return ctx.enter_context(nc.sbuf_tensor(name, shape, dt))

    def sem(name):
        return ctx.enter_context(nc.semaphore(name))

    def scratch(name, shape, dt=F32):
        return nc.dram_tensor(name, shape, dt).ap()

    with ctx:
        xn_dram = [scratch(f"xn_dram{n}", [T, H]) for n in range(2)]
        y_dram = [scratch(f"y_dram{n}", [T * TOPK, H]) for n in range(2)]
        q_dram = scratch("q_dram", [P, NT, H])
        bias_dram = scratch("bias_dram", [3, NB], BF16)

        xs = sb("xs", [P, NT, H], F32)
        up_w = [sb(f"up_{h}", [P, KC, E, F], F32R) for h in ("hi", "lo")]
        dn_w = [sb(f"dn_{h}", [P, KC, E, H], F32R) for h in ("hi", "lo")]
        qk_w = [sb(f"qk_{h}", [P, KC, 2 * H], F32R) for h in ("hi", "lo")]
        wv = sb("wv", [P, KC, H], F32)
        wo = sb("wo", [P, KC, H], F32)
        wr = sb("wr", [P, KC, E], F32)
        bvrow = sb("bvrow", [1, H], F32)
        biases = sb("biases", [P, NB], BF16)
        xT = [sb(f"xT_{h}", [P, 2, 2, KC, P], F32R) for h in ("hi", "lo")]
        aT = [sb(f"aT_{h}", [P, 2, KC, P], F32R) for h in ("hi", "lo")]
        cst = sb("cst", [P, NCONST], F32)
        ones = sb("ones", [P, P], BF16)
        upper = sb("upper", [P, P], BF16)
        logit = sb("logit", [P, NT, E], F32)
        gate = sb("gate", [P, TOPK, NT], F32)
        gidx = sb("gidx", [P, NS], U32)
        sidx = sb("sidx", [P, NS], U32)
        gslot = sb("gslot", [P, 2, 2], U32)
        sslot = sb("sslot", [P, 2, 2], U32)
        expert = sb("expert", [1, NS], I32)
        small = sb("small", [P, 48], F32)
        bst = sb("bst", [P, 2, 6], F32)
        sbmv = sb("sbmv", [P, 8], F32)
        work = sb("work", [P, WORK], F32)
        ps = ctx.enter_context(nc.psum_tensor("ps", [P, 8, 512], F32))

        ident = cst[:, C_ID:C_ID + P]

        def area(at, *shape, dt=F32):
            n = 1
            for d in shape:
                n *= d
            words = n if dt in (F32, U32, I32) else n // 2
            assert at + words <= WORK
            v = work[:, at:at + words]
            if dt is not F32:
                v = v.bitcast(dt)
            names = "abcd"[:len(shape)]
            if len(shape) == 1:
                return v
            return v.rearrange(f"p ({' '.join(names)}) -> p {' '.join(names)}",
                               **dict(zip(names[1:], shape[1:])))

        raw = area(3136, 2, 1536)
        iotaS = area(2048, P, QC, dt=BF16)
        iotaJ = area(2560, NS, QC, dt=BF16)
        qnum = area(2848, NS, QC, dt=BF16)
        xn_r = area(0, 2, 2, H)
        xTf = area(1024, 2, 2, KC, P)
        xg = area(0, 2, 2, H)
        glu = area(1024, 2, 2, I)
        upv = area(2048, 2, I)
        act_v = area(2560, 2, 2, I)
        ysb = area(3584, 2, 2, H)
        ybuf = area(0, 4, 2, TOPK, H)
        xn_a = area(4096, 4, 2, H + 2)
        qk = area(6160, 2, 2, 2 * H)
        rotr = area(8208, 2, 2 * HEADS, ROT)
        roti = area(8528, 2, 2 * HEADS, ROT)
        gsb = area(0, KC, H + 2)
        gT = area(516, KC, H)
        ksT = area(1028, H)
        sT = area(1284, KC, P)
        qin = area(3136, 4, 2, H)
        bstage = area(6208, 54)
        bparts = area(6272, 3, 54, dt=BF16)
        bres = area(6400, 54)
        iint = area(6464, 2 * 576, dt=I32)

        x_loaded = [sem(f"x_loaded{c}") for c in range(4)]
        consts_loaded = sem("consts_loaded")
        small_loaded = sem("small_loaded")
        raw_loaded = [sem(f"raw_loaded{b}") for b in range(2)]
        raw_hi = sem("raw_hi")
        raw_lo = sem("raw_lo")
        bias_loaded = sem("bias_loaded")
        bias_split = sem("bias_split")
        bias_stored = sem("bias_stored")
        bias_ready = sem("bias_ready")
        bias_zeroed = sem("bias_zeroed")
        consts_made = sem("consts_made")
        iotas_made = sem("iotas_made")
        dve_step = sem("dve_step")
        pool_step = sem("pool_step")
        pool_passed = sem("pool_passed")
        dve_passed = sem("dve_passed")

        class Layer:

            def __init__(self, n):
                s = lambda name: sem(f"{name}{n}")
                self.var, self.sd, self.xn = s("var"), s("sd"), s("xn")
                self.xn_stored = [s("xn_stored_a"), s("xn_stored_b")]
                self.xn_T, self.xn_Tsb, self.logits = s("xn_T"), s("xn_Tsb"), s("logits")
                self.mask, self.prefix, self.gap = s("mask"), s("prefix"), s("gap")
                self.gates, self.hot, self.hot_used = s("gates"), s("hot"), s("hot_used")
                self.slots, self.routed = s("slots"), s("routed")
                self.gathered = [s("gathered_a"), s("gathered_b")]
                self.scattered = [s("scattered_a"), s("scattered_b")]
                self.x_T, self.x_hi, self.x_lo = s("x_T"), s("x_hi"), s("x_lo")
                self.gu, self.glu, self.act, self.upd = s("gu"), s("glu"), s("act"), s("upd")
                self.a_T, self.a_hi, self.a_lo = s("a_T"), s("a_hi"), s("a_lo")
                self.y_ps, self.y_sb = s("y_ps"), s("y_sb")
                self.y_loaded = [s(f"y_loaded_{j}") for j in range(4)]
                self.logit_sb = s("logit_sb")
                self.y_used = s("y_used")

        L = [Layer(0), Layer(1)]
        A = Layer(2)
        qk_ps, qk_sb, rot_parts, rot_done = sem("qk_ps"), sem("qk_sb"), sem("rot_parts"), sem("rot_done")
        g_used = sem("g_used")
        q_stored = [sem("q_stored_a"), sem("q_stored_b")]
        q_loaded = [sem(f"q_loaded_{j}") for j in range(4)]
        mid_pe, mid_dve, m_hi, m_lo = sem("mid_pe"), sem("mid_dve"), sem("m_hi"), sem("m_lo")
        q_T, q_hi, q_lo, o_ps, x_done = sem("q_T"), sem("q_hi"), sem("q_lo"), sem("o_ps"), sem("x_done")
        out_ready, out_stored = sem("out_ready"), sem("out_stored")

        block = ctx.enter_context(nc.Block())
        x_v = x.rearrange("b (p i) h -> p (b i) h", p=P)
        out_v = out.rearrange("b (p i) h -> p (b i) h", p=P)
        xn_v = [d.rearrange("(p i) h -> p i h", p=P) for d in xn_dram]
        y_v = [d.rearrange("(p i k) h -> p i k h", p=P, k=TOPK) for d in y_dram]

        def pair(v, g):
            return v[:, bass.ds(g * 2, 2)]

        def hot(b):
            at = 3136 + b * 1376
            return area(at, P, QC, dt=BF16), area(at + 512, NS, QC, dt=BF16), area(at + 800, NS, QC, dt=BF16)

        @block.sync
        def _(sp):
            sp.dma_start(cst[:, :], consts).then_inc(consts_loaded, 16)
            for c in range(4):
                sp.dma_start(xs[:, 8 * c:8 * c + 8, :], x_v[:, 8 * c:8 * c + 8, :]).then_inc(x_loaded[c], 16)

            def load_raw(e, b):
                sp.dma_start(raw[:, b, 0:KC * F].rearrange("p (c f) -> p c f", c=KC),
                             Wup[bass.ds(e, 1)].rearrange("a (c p) f -> p (a c) f", p=P)).then_inc(raw_loaded[b], 16)
                sp.dma_start(raw[:, b, KC * F:KC * (F + H)].rearrange("p (c f) -> p c f", c=KC),
                             Wdn[bass.ds(e, 1)].rearrange("a (c p) f -> p (a c) f", p=P)).then_inc(raw_loaded[b], 16)

            for e in range(2):
                load_raw(e, e)
            sp.wait_ge(bias_split, 1)
            for at, n, col in ((0, 32, B_UP), (32, 16, B_DN), (48, 2, B_QK), (50, 2, B_QK + H), (52, 2, B_O)):
                sp.dma_start(bias_dram[:, col:col + P * n].rearrange("k (p c) -> p k c", p=P),
                             bparts[:, :, at:at + n]).then_inc(bias_stored, 16)
            sp.wait_ge(bias_stored, 16 * 5)
            sp.wait_ge(bias_zeroed, 1)
            sp.dma_start(biases[0:3, :], bias_dram[:, :]).then_inc(bias_ready, 16)
            with sp.Fori(1, E // 2) as it:
                for b in range(2):
                    sp.wait_ge(raw_lo, it * 2 + b - 1)
                    load_raw(it * 2 + b, b)
            sp.wait_ge(raw_lo, E - 1)
            for w, c in ((Wq, 0), (Wk, H)):
                sp.dma_start(raw[:, 0, 0:KC * 2 * H].rearrange("p (c f) -> p c f", c=KC)[:, :, c:c + H],
                             w.rearrange("(c p) f -> p c f", p=P)).then_inc(raw_loaded[0], 16)

            def wait_scattered(n):
                for b in range(2):
                    sp.wait_ge(L[n].scattered[b], 32 * (NP // 2))

            wait_scattered(0)
            for j in range(4):
                sp.dma_start(ybuf[:, j], pair(y_v[0], j)).then_inc(L[0].y_loaded[j], 16)
            with sp.Fori(0, NG // 4 - 1) as it:
                for j in range(4):
                    g = it * 4 + j
                    sp.wait_ge(L[0].y_used, g + 1)
                    sp.dma_start(ybuf[:, j], pair(y_v[0], g + 4)).then_inc(L[0].y_loaded[j], 16)

            for b in range(2):
                sp.wait_ge(q_stored[b], 16 * (NG // 2))
            sp.wait_ge(g_used, NG)
            for j in range(4):
                sp.dma_start(qin[:, j], pair(q_dram, j)).then_inc(q_loaded[j], 16)
            with sp.Fori(0, NG // 4 - 1) as it:
                for j in range(4):
                    g = it * 4 + j
                    sp.wait_ge(q_T, g + 1)
                    sp.dma_start(qin[:, j], pair(q_dram, g + 4)).then_inc(q_loaded[j], 16)

            wait_scattered(1)
            for j in range(4):
                sp.dma_start(ybuf[:, j], pair(y_v[1], j)).then_inc(L[1].y_loaded[j], 16)

            def finish(g, j, more):
                sp.wait_ge(L[1].y_used, g + 1)
                if more:
                    sp.dma_start(ybuf[:, j], pair(y_v[1], g + 4)).then_inc(L[1].y_loaded[j], 16)
                sp.dma_start(pair(out_v, g), pair(xs, g)).then_inc(out_stored, 16)

            with sp.Fori(0, NG // 4 - 1) as it:
                for j in range(4):
                    finish(it * 4 + j, j, True)
            for j in range(4):
                finish(NG - 4 + j, j, False)
            sp.wait_ge(out_stored, 16 * NG)

        @block.gpsimd
        def _(pool):
            st = Steps(pool, pool_step, pool_passed)
            pool.dma_start(wr[:, :, :], Wr.rearrange("(c p) e -> p c e", p=P)).then_inc(small_loaded, 16)
            pool.dma_start(wv[:, :, :], Wv.rearrange("(c p) o -> p c o", p=P)).then_inc(small_loaded, 16)
            pool.dma_start(wo[:, :, :], Wo.rearrange("(c p) o -> p c o", p=P)).then_inc(small_loaded, 16)
            pool.dma_start(bvrow[:, :], bv.rearrange("(a o) -> a o", a=1)).then_inc(small_loaded, 16)

            def make_iotas():
                for k, (dst, n, pattern, base) in enumerate((
                        (iotaS, P, [[1, P // 2], [0, QC]], 0),
                        (iotaS, P, [[1, P // 2], [0, QC]], P // 2),
                        (iotaJ, NS, [[1, NS], [0, QC]], 0), (qnum, NS, [[0, NS], [1, QC]], 1))):
                    n2 = pattern[0][1]
                    st.done(nc.gpsimd.iota(iint[:, 0:n2 * QC], pattern=pattern, base=base, channel_multiplier=0))
                    d = dst[:, base:base + n2, :] if n == P else dst[:, :, :]
                    st.done(nc.gpsimd.tensor_copy(d, iint[:, 0:n2 * QC].rearrange("p (a b) -> p a b", b=QC)))

            make_iotas()
            nc.gpsimd.memset(biases[:, :], 0.0).then_inc(bias_zeroed, 1)
            pool.sem_inc(iotas_made, 1)

            def low(c, b, parts):
                pool.wait_ge(raw_hi, c + 1)
                for j, (dst, src, hi) in enumerate(parts):
                    ins = nc.gpsimd.tensor_tensor(dst, src, hi.bitcast(F32), ALU.subtract)
                ins.then_inc(raw_lo, 1)

            def expert_parts(e, b, h):
                u, d = raw[:, b, 0:KC * F], raw[:, b, KC * F:KC * (F + H)]
                return ((up_w[h][:, :, bass.ds(e, 1), :].rearrange("p c a f -> p c (a f)"),
                         u.rearrange("p (c f) -> p c f", c=KC)),
                        (dn_w[h][:, :, bass.ds(e, 1), :].rearrange("p c a f -> p c (a f)"),
                         d.rearrange("p (c f) -> p c f", c=KC)))

            def body(it):
                for b in range(2):
                    e = it * 2 + b
                    low(e, b, [(lo, src, hi) for (lo, src), (hi, _) in
                               zip(expert_parts(e, b, 1), expert_parts(e, b, 0))])
            repeat(pool, E // 2, body)
            low(E, 0, [(qk_w[1][:, :, :], raw[:, 0, 0:KC * 2 * H].rearrange("p (c f) -> p c f", c=KC),
                        qk_w[0][:, :, :])])

            def experts(n):
                l = L[n]
                for b in range(2):
                    pool.wait_ge(l.xn_stored[b], 16 * (NG // 2))
                pool.wait_ge(l.routed, 1)

                def gather(s, b):
                    st.hold()
                    st.done(nc.gpsimd.tensor_copy(gslot[:, b, :], gidx[:, bass.ds(s * 2, 2)]))
                    st.hold()
                    for u in range(2):
                        pool.indirect_dma_start(xg[:, b, u, :], None, xn_dram[n],
                                                bass.IndirectOffsetOnAxis(ap=gslot[:, b, u:u + 1], axis=0)
                                                ).then_inc(l.gathered[b], 16)

                def scatter(s, b, k):
                    pool.wait_ge(l.y_sb, s + 1)
                    wait(pool, l.scattered[b], 32 * k)
                    st.hold()
                    st.done(nc.gpsimd.tensor_copy(sslot[:, b, :], sidx[:, bass.ds(s * 2, 2)]))
                    st.hold()
                    for u in range(2):
                        pool.indirect_dma_start(y_dram[n], bass.IndirectOffsetOnAxis(ap=sslot[:, b, u:u + 1], axis=0),
                                                ysb[:, b, u, :], None, bounds_check=T * TOPK - 1,
                                                oob_is_err=False).then_inc(l.scattered[b], 16)

                for s in range(2):
                    gather(s, s)
                for s in range(2, 6):
                    pool.wait_ge(l.x_T, s - 1)
                    gather(s, s % 2)

                def body(it):
                    for b in range(2):
                        s = it * 2 + b
                        scatter(s, b, it)
                        pool.wait_ge(l.x_T, s + 5)
                        gather(s + 6, b)
                st.loop((NP - 6) // 2, 4, body)
                for s in range(NP - 6, NP):
                    scatter(s, s % 2, s // 2)

            experts(0)

            def rotation_sums(g, b):
                v = qk[:, b].rearrange("p u (h j c) -> p u h j c", j=HD // 2, c=2)
                pool.wait_ge(rot_parts, g + 1)
                r, i = v[:, :, :, 0:ROT, 0], v[:, :, :, 0:ROT, 1]
                for u in range(2):
                    nc.gpsimd.tensor_tensor(r[:, u], r[:, u], rotr[:, u], ALU.subtract)
                for u in range(2):
                    ins = nc.gpsimd.tensor_tensor(i[:, u], i[:, u], roti[:, u], ALU.add)
                ins.then_inc(rot_done, 1)

            def body(it):
                for b in range(2):
                    rotation_sums(it * 2 + b, b)
            repeat(pool, NG // 2, body)
            pool.wait_ge(mid_dve, 4)
            for b in range(2):
                pool.wait_ge(q_stored[b], 16 * (NG // 2))
            make_iotas()
            pool.sem_inc(iotas_made, 1)
            experts(1)

        @block.scalar
        def _(act):
            segs = ((bup.rearrange("e f -> (e f)"), 0, 32), (bdn.rearrange("e f -> (e f)"), 32, 16),
                    (bq, 48, 2), (bk, 50, 2), (bo, 52, 2))
            for src, at, n in segs:
                act.dma_start(bstage[:, at:at + n], src.rearrange("(p c) -> p c", p=P)).then_inc(bias_loaded, 16)

            def high(e, b, k):
                act.wait_ge(raw_loaded[b], 32 * (k + 1))
                nc.scalar.activation(up_w[0][:, :, bass.ds(e, 1), :].rearrange("p c a f -> p c (a f)"),
                                     raw[:, b, 0:KC * F].rearrange("p (c f) -> p c f", c=KC), ACT.Copy)
                nc.scalar.activation(dn_w[0][:, :, bass.ds(e, 1), :].rearrange("p c a f -> p c (a f)"),
                                     raw[:, b, KC * F:KC * (F + H)].rearrange("p (c f) -> p c f", c=KC),
                                     ACT.Copy).then_inc(raw_hi, 1)

            def sqrt_var(l, b, g):
                act.wait_ge(l.var, g + 1)
                nc.scalar.activation(small[:, 8 + 2 * b:10 + 2 * b], small[:, 4 + 2 * b:6 + 2 * b],
                                     ACT.Sqrt).then_inc(l.sd, 1)

            def xn_out(l, n, g, b):
                act.wait_ge(l.xn_T, g + 1)
                act.dma_start(pair(xn_v[n], g), xn_r[:, b]).then_inc(l.xn_stored[b], 16)
                nc.scalar.activation(xTf[:, b], ps[:, b, :].rearrange("p (u c t) -> p u c t", u=2, c=KC),
                                     ACT.Copy).then_inc(l.xn_Tsb, 1)

            def logits_out(l, g, b):
                act.wait_ge(l.logits, g + 1)
                nc.scalar.activation(pair(logit, g), ps[:, 6 + b, 0:2 * E].rearrange("p (u e) -> p u e", u=2),
                                     ACT.Copy).then_inc(l.logit_sb, 1)

            def norm_step(l, n, g, b, first=False, last=False):
                if not last:
                    sqrt_var(l, 1 - b, g + 1)
                xn_out(l, n, g, b)
                if not first:
                    logits_out(l, g - 1, 1 - b)

            sqrt_var(L[0], 0, 0)

            def first_norm(g, j, it):
                static = isinstance(g, int)
                norm_step(L[0], 0, g, j % 2, first=static and g == 0, last=static and g == NG - 1)
                if j % 2:
                    high(it * 2 + j // 2, j // 2, it)
            stages(act, first_norm)
            logits_out(L[0], NG - 1, 1)
            act.wait_ge(raw_loaded[0], 32 * (E // 2 + 1))
            nc.scalar.activation(qk_w[0][:, :, :], raw[:, 0, 0:KC * 2 * H].rearrange("p (c f) -> p c f", c=KC),
                                 ACT.Copy).then_inc(raw_hi, 1)

            def gates(l):
                act.wait_ge(l.gap, 1)
                nc.scalar.activation(gate[:, 1, :], small[:, 16:16 + NT], ACT.Sigmoid)
                nc.scalar.activation(gate[:, 0, :], small[:, 16:16 + NT], ACT.Sigmoid, scale=-1.0).then_inc(l.gates, 1)

            def experts(l):
                def x_hi(s, b):
                    act.wait_ge(l.x_T, s + 1)
                    nc.scalar.activation(xT[0][:, b], ps[:, b, :].rearrange("p (u c t) -> p u c t", u=2, c=KC),
                                         ACT.Copy).then_inc(l.x_hi, 1)

                def a_hi(s):
                    act.wait_ge(l.a_T, s + 1)
                    nc.scalar.activation(aT[0][:, :, :, :], ps[:, 6, :].rearrange("p (u c t) -> p u c t", u=2, c=KC),
                                         ACT.Copy).then_inc(l.a_hi, 1)

                def glus(s, b):
                    wait(act, l.act, s - 1)
                    for u in range(2):
                        act.wait_ge(l.gu, s * 2 + u + 1)
                        nc.scalar.activation(glu[:, b, u, :],
                                             ps[:, 2 + 2 * b + u, :].rearrange("p (f c) -> p f c", c=2)[:, :, 0],
                                             ACT.Gelu_apprx_sigmoid).then_inc(l.glu, 1)

                def y_out(s, b, k):
                    act.wait_ge(l.y_ps, s + 1)
                    wait(act, l.scattered[b], 32 * k)
                    nc.scalar.activation(ysb[:, b], ps[:, 7, :].rearrange("p (u h) -> p u h", u=2),
                                         ACT.Copy).then_inc(l.y_sb, 1)

                x_hi(0, 0)
                x_hi(1, 1)
                glus(0, 0)
                def body(it):
                    for d in range(2):
                        s, b = it * 2 + 1 + d, (1 + d) % 2
                        x_hi(s + 1, 1 - b)
                        a_hi(s - 1)
                        glus(s, b)
                        y_out(s - 1, 1 - b, it)
                repeat(act, NP // 2 - 1, body)
                a_hi(NP - 2)
                glus(NP - 1, 1)
                y_out(NP - 2, 0, NP // 2 - 1)
                a_hi(NP - 1)
                y_out(NP - 1, 1, NP // 2 - 1)

            gates(L[0])
            experts(L[0])

            def xT_high(g, b):
                act.wait_ge(A.x_T, g + 1)
                nc.scalar.activation(xT[0][:, b], ps[:, b, :].rearrange("p (u c t) -> p u c t", u=2, c=KC),
                                     ACT.Copy).then_inc(A.x_hi, 1)

            def qk_out(g, b, k):
                act.wait_ge(qk_ps, g + 1)
                wait(act, q_stored[b], 16 * k)
                nc.scalar.activation(qk[:, b], ps[:, 2 + 2 * b:4 + 2 * b, :], ACT.Copy).then_inc(qk_sb, 1)

            def store_q(g, b):
                act.wait_ge(rot_done, g + 1)
                act.dma_start(pair(q_dram, g), qk[:, b, :, 0:H]).then_inc(q_stored[b], 16)

            def first_pass(g, j, it):
                b = j % 2
                xT_high(g, b)
                if not (isinstance(g, int) and g == NG - 1):
                    sqrt_var(A, 1 - b, g + 1)
                if not (isinstance(g, int) and g < 2):
                    store_q(g - 2, b)
                if not (isinstance(g, int) and g < 1):
                    qk_out(g - 1, 1 - b, it * 2 + (j - 1) // 2)

            sqrt_var(A, 0, 0)
            stages(act, first_pass)
            store_q(NG - 2, 0)
            qk_out(NG - 1, 1, NG // 2 - 1)
            store_q(NG - 1, 1)

            act.wait_ge(mid_pe, 4)
            nc.scalar.activation(qk_w[0][:, :, 0:H], ps[:, 4, :].rearrange("p (a o) -> p a o", a=KC),
                                 ACT.Copy).then_inc(m_hi, 1)

            def q_high(g, b):
                act.wait_ge(q_T, g + 1)
                nc.scalar.activation(xT[0][:, b], ps[:, 2 + b, :].rearrange("p (u c t) -> p u c t", u=2, c=KC),
                                     ACT.Copy).then_inc(q_hi, 1)

            q_high(0, 0)
            q_high(1, 1)
            q_high(2, 0)
            sqrt_var(L[1], 0, 0)

            def second_pass(g, j, it):
                b = j % 2
                static = isinstance(g, int)
                if not (static and g + 3 >= NG):
                    q_high(g + 3, 1 - b)
                norm_step(L[1], 1, g, b, first=static and g == 0, last=static and g == NG - 1)
            stages(act, second_pass)
            logits_out(L[1], NG - 1, 1)
            gates(L[1])
            experts(L[1])

        @block.tensor
        def _(pe):
            def transpose4(bank, src):
                for u in range(2):
                    for c in range(KC):
                        k = (u * KC + c) * P
                        ins = nc.tensor.transpose(ps[:, bank, k:k + P], src[:, u, c * P:(c + 1) * P], ident)
                return ins

            def bias(out, at, width, start=True):
                nc.tensor.matmul(out, ones[:, :], biases[:, bass.ds(at, width)], start=True, stop=False)

            def product(out, st_hi, st_lo, mv_hi, mv_lo, stop):
                nc.tensor.matmul(out, st_hi, mv_hi, start=False, stop=False)
                nc.tensor.matmul(out, st_hi, mv_lo, start=False, stop=False)
                return nc.tensor.matmul(out, st_lo, mv_hi, start=False, stop=stop)

            pe.wait_ge(consts_loaded, 16)
            pe.wait_ge(consts_made, 1)
            pe.wait_ge(small_loaded, 64)

            def xn_transpose(l, g, b):
                pe.wait_ge(l.xn, g + 1)
                transpose4(b, xn_r[:, b]).then_inc(l.xn_T, 1)

            def logits(l, g, b):
                pe.wait_ge(l.xn_Tsb, g + 1)
                for u in range(2):
                    for c in range(KC):
                        ins = nc.tensor.matmul(ps[:, 6 + b, u * E:(u + 1) * E], xTf[:, b, u, c, :],
                                               wr[:, c, :], start=(c == 0), stop=(c == KC - 1))
                ins.then_inc(l.logits, 1)

            def layer_norm_loop(l):
                xn_transpose(l, 0, 0)
                def body(it):
                    for b in range(2):
                        g = it * 2 + b
                        xn_transpose(l, g + 1, 1 - b)
                        logits(l, g, b)
                repeat(pe, NG // 2 - 1, body)
                xn_transpose(l, NG - 1, 1)
                logits(l, NG - 2, 0)
                logits(l, NG - 1, 1)

            def route(l):
                pe.wait_ge(l.mask, 1)
                m = area(0, 256, dt=BF16)
                nc.tensor.matmul(ps[:, 2, 0:NT * E], upper[:, :], m, start=True, stop=True)
                nc.tensor.matmul(ps[:, 2, NT * E:2 * NT * E], ones[:, :], m, start=True, stop=True).then_inc(l.prefix, 1)
                for c in range(NQC):
                    pe.wait_ge(l.hot, c + 1)
                    hs, hc, hp = hot(c % 2)
                    for k in range(QC):
                        first, last = c == 0 and k == 0, c == NQC - 1 and k == QC - 1
                        nc.tensor.matmul(ps[:, 3, 0:NS], hs[:, :, k], hc[:, :, k], start=first, stop=last)
                        ins = nc.tensor.matmul(ps[:, 4, 0:NS], hs[:, :, k], hp[:, :, k], start=first, stop=last)
                    ins.then_inc(l.hot_used, 1)

            names = [[pe.alloc_register(f"expert_{b}{u}") for u in range(2)] for b in range(2)]

            def experts(l):
                pe.wait_ge(l.routed, 1)
                pe.wait_ge(raw_lo, E + 1)
                pe.wait_ge(raw_hi, E + 1)
                pe.wait_ge(bias_ready, 16)

                def load_names(s, b):
                    pe.load(names[b], expert[0:1, bass.ds(s * 2, 2)])

                def named(b):
                    return [pe.snap(r, min_val=0, max_val=E - 1) for r in names[b]]

                def x_transpose(s, b, k):
                    pe.wait_ge(l.gathered[b], 32 * (k + 1))
                    transpose4(b, xg[:, b]).then_inc(l.x_T, 1)

                def up(s, b, u, e):
                    if u == 0:
                        pe.wait_ge(l.x_lo, s + 1)
                    else:
                        wait(pe, l.y_sb, s - 1)
                    o = ps[:, 2 + 2 * b + u, :]
                    bias(o, e * F + B_UP, F)
                    for c in range(KC):
                        ins = product(o, xT[0][:, b, u, c, :], xT[1][:, b, u, c, :],
                                      up_w[0][:, c, bass.ds(e, 1), :], up_w[1][:, c, bass.ds(e, 1), :], c == KC - 1)
                    ins.then_inc(l.gu, 1)

                def a_transpose(s, b):
                    pe.wait_ge(l.act, s + 1)
                    transpose4(6, act_v[:, b]).then_inc(l.a_T, 1)

                def down(s, e):
                    pe.wait_ge(l.a_lo, s + 1)
                    for u in range(2):
                        o = ps[:, 7, u * H:(u + 1) * H]
                        bias(o, e[u] * H + B_DN, H)
                        for c in range(KC):
                            ins = product(o, aT[0][:, u, c, :], aT[1][:, u, c, :],
                                          dn_w[0][:, c, bass.ds(e[u], 1), :], dn_w[1][:, c, bass.ds(e[u], 1), :],
                                          c == KC - 1)
                    ins.then_inc(l.y_ps, 1)

                x_transpose(0, 0, 0)
                x_transpose(1, 1, 0)
                load_names(0, 0)
                load_names(1, 1)
                e = named(0)
                for u in range(2):
                    up(0, 0, u, e[u])
                def body(it):
                    for d in range(2):
                        s, b = it * 2 + 1 + d, (1 + d) % 2
                        x_transpose(s + 1, 1 - b, it + 1)
                        e, e_last = named(b), named(1 - b)
                        up(s, b, 0, e[0])
                        load_names(s + 1, 1 - b)
                        a_transpose(s - 1, 1 - b)
                        up(s, b, 1, e[1])
                        down(s - 1, e_last)
                repeat(pe, NP // 2 - 1, body)
                e, e_last = named(1), named(0)
                up(NP - 1, 1, 0, e[0])
                a_transpose(NP - 2, 0)
                up(NP - 1, 1, 1, e[1])
                down(NP - 2, e_last)
                a_transpose(NP - 1, 1)
                pe.wait_ge(l.y_sb, NP - 1)
                down(NP - 1, e)

            layer_norm_loop(L[0])
            route(L[0])
            experts(L[0])

            def a_in(g, j):
                pe.wait_ge(A.xn, g + 1)
                transpose4(j % 2, xn_a[:, j]).then_inc(A.x_T, 1)

            def project(g, b):
                for u in range(2):
                    o = ps[:, 2 + 2 * b + u, :]
                    if u == 0:
                        pe.wait_ge(A.x_lo, g + 1)
                    bias(o, B_QK, 2 * H)
                    for c in range(KC):
                        ins = product(o, xT[0][:, b, u, c, :], xT[1][:, b, u, c, :], qk_w[0][:, c, :], qk_w[1][:, c, :],
                                      c == KC - 1)
                ins.then_inc(qk_ps, 1)

            def key_sums(g, j, first=False, last=False):
                pe.wait_ge(rot_done, g + 1)
                for u in range(2):
                    for a in range(KC):
                        k = H + a * P
                        ins = nc.tensor.matmul(ps[:, 6 + a, 0:H + 2], qk[:, j % 2, u, k:k + P], xn_a[:, j, u, :],
                                               start=first and u == 0, stop=last and u == 1, skip_group_check=True)
                ins.then_inc(g_used, 1)

            def first_pass(g, j, it):
                static = isinstance(g, int)
                a_in(g, j)
                if not (static and g < 3):
                    key_sums(g - 3, (j + 1) % 4, first=static and g == 3)
                if not (static and g < 1):
                    project(g - 1, (j + 1) % 2)
            stages(pe, first_pass)
            key_sums(NG - 3, (NG - 3) % 4)
            project(NG - 1, 1)
            key_sums(NG - 2, (NG - 2) % 4)
            key_sums(NG - 1, (NG - 1) % 4, last=True)

            pe.wait_ge(mid_dve, 1)
            for c in range(KC):
                for a in range(KC):
                    nc.tensor.transpose(ps[:, 2, (c * KC + a) * P:(c * KC + a + 1) * P],
                                        gsb[:, a, c * P:(c + 1) * P], ident)
            for a in range(KC):
                ins = nc.tensor.transpose(ps[0:2, 3, a * P:(a + 1) * P], gsb[:, a, H:H + 2], ident)
            ins.then_inc(mid_pe, 1)
            pe.wait_ge(mid_dve, 2)
            for a in range(KC):
                o = ps[:, 5, a * P:(a + 1) * P]
                for c in range(KC):
                    nc.tensor.matmul(o, wv[:, c, a * P:(a + 1) * P], gT[:, c, a * P:(a + 1) * P],
                                     start=(c == 0), stop=False)
                ins = nc.tensor.matmul(o, bvrow[0:1, a * P:(a + 1) * P], ksT[0:1, a * P:(a + 1) * P],
                                       start=False, stop=True)
            ins.then_inc(mid_pe, 2)
            pe.wait_ge(mid_dve, 3)
            for a in range(KC):
                ins = nc.tensor.matmul(ps[:, 4, a * H:(a + 1) * H], sT[:, a, :], wo[:, a, :], start=True, stop=True)
            ins.then_inc(mid_pe, 1)

            def q_transpose(g, j, k):
                pe.wait_ge(q_loaded[j], 16 * (k + 1))
                transpose4(2 + j % 2, qin[:, j]).then_inc(q_T, 1)

            def attend(g, b):
                for u in range(2):
                    o = ps[:, 4 + b, u * H:(u + 1) * H]
                    if u == 0:
                        wait(pe, x_done, g - 1)
                    bias(o, B_O, H)
                    if u == 0:
                        pe.wait_ge(q_lo, g + 1)
                    for a in range(KC):
                        ins = product(o, xT[0][:, b, u, a, :], xT[1][:, b, u, a, :], qk_w[0][:, a, 0:H],
                                      qk_w[1][:, a, 0:H], a == KC - 1)
                ins.then_inc(o_ps, 1)

            pe.wait_ge(mid_dve, 4)
            q_transpose(0, 0, 0)
            q_transpose(1, 1, 0)
            pe.wait_ge(m_lo, 1)
            attend(0, 0)
            q_transpose(2, 2, 0)
            attend(1, 1)
            l = L[1]

            def second_pass(g, j, it):
                b, static = j % 2, isinstance(g, int)
                if not (static and g + 2 >= NG):
                    attend(g + 2, b)
                if not (static and g + 3 >= NG):
                    q_transpose(g + 3, (j + 3) % 4, it + (j + 3) // 4)
                xn_transpose(l, g, b)
                if not (static and g < 1):
                    logits(l, g - 1, 1 - b)
            stages(pe, second_pass)
            logits(l, NG - 1, 1)
            route(l)
            experts(l)

        @block.vector
        def _(dve):
            v = nc.vector
            st = Steps(dve, dve_step, dve_passed)
            dve.wait_ge(consts_loaded, 16)
            v.memset(ones[:, :], 1.0)
            v.tensor_copy(upper[:, :], cst[:, C_UP:C_UP + P]).then_inc(consts_made, 1)

            def split_biases():
                dve.wait_ge(bias_loaded, 80)
                odd = bstage[:, 0:32].rearrange("p (f c) -> p f c", c=2)[:, :, 1]
                st.done(v.tensor_scalar(odd, odd, 1.0, None, ALU.add))
                st.done(v.tensor_copy(bparts[:, 0, :], bstage[:, :]))
                st.done(v.tensor_tensor(bres[:, :], bstage[:, :], bparts[:, 0, :], ALU.subtract))
                st.done(v.tensor_copy(bparts[:, 1, :], bres[:, :]))
                st.done(v.tensor_tensor(bres[:, :], bres[:, :], bparts[:, 1, :], ALU.subtract))
                v.tensor_copy(bparts[:, 2, :], bres[:, :]).then_inc(bias_split, 1)

            mv = [[sbmv[:, 4 * b + 2 * u:4 * b + 2 * u + 2] for u in range(2)] for b in range(2)]

            def moments(l, g, b):
                st.hold()
                for u in range(2):
                    ins = v.bn_stats(bst[:, u, :], xs[:, bass.ds(g * 2 + u, 1), :].rearrange("p a h -> p (a h)"))
                st.done(ins)
                st.hold()
                for u in range(2):
                    ins = v.bn_aggr(mv[b][u], bst[:, u, :])
                st.done(ins)
                v.tensor_scalar(small[:, 4 + 2 * b:6 + 2 * b],
                                sbmv[:, 4 * b:4 * b + 4].rearrange("p (u c) -> p u c", c=2)[:, :, 1],
                                EPS, None, ALU.add).then_inc(l.var, 1)

            def normalise(l, dst, g, b):
                dve.wait_ge(l.sd, g + 1)
                st.done(v.reciprocal(small[:, 12 + 2 * b:14 + 2 * b], small[:, 8 + 2 * b:10 + 2 * b]))
                for u in range(2):
                    ins = v.tensor_scalar(dst[:, u, 0:H], xs[:, bass.ds(g * 2 + u, 1), :].rearrange("p a h -> p (a h)"),
                                          mv[b][u][:, 0:1], small[:, 12 + 2 * b + u:13 + 2 * b + u],
                                          ALU.subtract, ALU.mult)
                ins.then_inc(l.xn, 1)

            l = L[0]
            dve.wait_ge(x_loaded[0], 16)
            moments(l, 0, 0)

            def ln_step(g, j, it):
                b, static = j % 2, isinstance(g, int)
                if static and g == 3:
                    for c in range(1, 4):
                        dve.wait_ge(x_loaded[c], 16)
                    split_biases()
                k = it * 2 + j // 2
                wait(dve, l.xn_stored[b], 16 * k)
                normalise(l, xn_r[:, b], g, b)
                if not (static and g + 1 >= NG):
                    moments(l, g + 1, 1 - b)
            st.stages(12, ln_step)

            def route(n):
                l = L[n]
                mask = area(0, NT * E, dt=BF16)
                lg = logit[:, :, :]
                eq = area(512, NT, E)
                cand = area(768, NT, E)
                oh = [area(1024 + 256 * k, NT, E) for k in range(2)]
                prod = area(1536, NT, E)
                scan = [area(6208 + 400 * k, PAD + NT, E) for k in range(2)]
                top = area(7040, 2, NT)
                pick = area(7104, NT)
                pos = area(7136, NT, TOPK)
                posi = area(7200, 2, NQ, dt=I32)
                posb = area(7328, 2, NQ, dt=BF16)
                tiles = area(7400, 2, 16)
                tilei = area(7440, 16, dt=I32)
                nam = area(7460, 2, NS)
                cmp = area(512, NS, E)
                dve.wait_ge(l.logit_sb, NG)
                dve.wait_ge(iotas_made, n + 1)
                if n == 0:
                    dve.wait_ge(raw_lo, E + 1)
                    dve.wait_ge(bias_ready, 16)
                for b in range(2):
                    dve.wait_ge(l.xn_stored[b], 16 * (NG // 2))
                eiota = cst[:, None, C_E:C_E + E].to_broadcast([P, NT, E])
                for k in range(TOPK):
                    st.done(v.tensor_reduce(top[:, k, :], lg, AX.X, ALU.max))
                    st.done(v.tensor_tensor(eq, lg, top[:, k, :, None].to_broadcast([P, NT, E]), ALU.is_equal))
                    st.done(v.scalar_tensor_tensor(out=cand, in0=eq, scalar=-float(E), in1=eiota,
                                                   op0=ALU.mult, op1=ALU.add))
                    st.done(v.tensor_reduce(pick, cand, AX.X, ALU.min))
                    st.done(v.tensor_tensor(oh[k], cand, pick[:, :, None].to_broadcast([P, NT, E]), ALU.is_equal))
                    if k == 0:
                        st.done(v.scalar_tensor_tensor(out=lg, in0=oh[0], scalar=MASKED, in1=lg,
                                                       op0=ALU.mult, op1=ALU.add))
                v.tensor_tensor(small[:, 16:16 + NT], top[:, 1, :], top[:, 0, :], ALU.subtract).then_inc(l.gap, 1)
                v.tensor_tensor(mask.rearrange("p (i e) -> p i e", e=E), oh[0], oh[1], ALU.add).then_inc(l.mask, 1)
                for k in range(2):
                    st.done(v.memset(scan[k][:, 0:PAD, :], 0.0))
                v.memset(tiles[:, :, 0:8], 0.0)
                dve.wait_ge(l.prefix, 1)
                st.done(v.tensor_copy(scan[0][:, PAD:, :],
                                      ps[:, 2, NT * E:2 * NT * E].rearrange("p (i e) -> p i e", e=E)))
                a = 0
                for d in (1, 2, 4, 8, 16):
                    st.done(v.tensor_tensor(scan[1 - a][:, PAD:, :], scan[a][:, PAD:, :],
                                            scan[a][:, PAD - d:PAD + NT - d, :], ALU.add))
                    a = 1 - a
                st.done(v.tensor_scalar(tilei[:, 0:E], scan[a][:, PAD + NT - 1, :], float(P - 1), None, ALU.add))
                st.done(v.tensor_single_scalar(tilei[:, 0:E], tilei[:, 0:E], 7, ALU.logical_shift_right))
                st.done(v.tensor_copy(tiles[:, 0, 8:16], tilei[:, 0:E]))
                c = 0
                for d in (1, 2, 4):
                    st.done(v.tensor_tensor(tiles[:, 1 - c, 8:16], tiles[:, c, 8:16], tiles[:, c, 8 - d:16 - d],
                                            ALU.add))
                    c = 1 - c
                before = tiles[:, c, 7:15]
                st.done(v.tensor_tensor(prod, ps[:, 2, 0:NT * E].rearrange("p (i e) -> p i e", e=E),
                                        scan[a][:, PAD - 1:PAD + NT - 1, :], ALU.add))
                st.done(v.scalar_tensor_tensor(out=prod, in0=before[:, None, :].to_broadcast([P, NT, E]), scalar=float(P),
                                               in1=prod, op0=ALU.mult, op1=ALU.add))
                for k in range(TOPK):
                    st.done(v.tensor_tensor(oh[k], oh[k], prod, ALU.mult))
                    st.done(v.tensor_reduce(pos[:, :, k], oh[k], AX.X, ALU.add))
                st.done(v.tensor_copy(posi[:, 1, :], pos.rearrange("p i k -> p (i k)")))
                st.done(v.tensor_single_scalar(posi[:, 0, :], posi[:, 1, :], 7, ALU.logical_shift_right))
                st.done(v.tensor_single_scalar(posi[:, 1, :], posi[:, 1, :], P - 1, ALU.bitwise_and))
                st.done(v.tensor_copy(posb, posi))
                row = slice(0, 1)
                st.done(v.tensor_tensor(cmp[row, :, 1:E], before[row, None, 1:E].to_broadcast([1, NS, E - 1]),
                                        iotaJ[row, :, 0:1].to_broadcast([1, NS, E - 1]), ALU.is_le))
                st.done(v.tensor_reduce(nam[row, 0, :], cmp[row, :, 1:E], AX.X, ALU.add))
                st.done(v.tensor_copy(expert[:, :], nam[row, 0, :]))
                for ch in range(NQC):
                    if ch >= 2:
                        dve.wait_ge(l.hot_used, ch - 1)
                    hs, hc, hp = hot(ch % 2)
                    cols = slice(ch * QC, (ch + 1) * QC)
                    st.done(v.tensor_tensor(hp, iotaJ, posb[:, 0, None, cols].to_broadcast([P, NS, QC]), ALU.is_equal))
                    v.tensor_tensor(hs, iotaS, posb[:, 1, None, cols].to_broadcast([P, P, QC]), ALU.is_equal)
                    st.done(v.scalar_tensor_tensor(out=hc, in0=qnum, scalar=float(ch * QC), in1=hp,
                                                   op0=ALU.add, op1=ALU.mult))
                    v.tensor_scalar(hp, hp, cst[:, C_P:C_P + 1], None, ALU.mult).then_inc(l.hot, 1)
                dve.wait_ge(l.hot_used, NQC)
                st.done(v.tensor_copy(nam[:, 1, :], ps[:, 3, 0:NS]))
                st.done(v.scalar_tensor_tensor(out=nam[:, 1, :], in0=ps[:, 4, 0:NS], scalar=float(NQ),
                                               in1=nam[:, 1, :], op0=ALU.mult, op1=ALU.add))
                st.done(v.tensor_scalar(nam[:, 0, :], nam[:, 1, :], 0.0, SKIP, ALU.is_equal, ALU.mult))
                v.scalar_tensor_tensor(out=sidx[:, :], in0=nam[:, 1, :], scalar=-1.0, in1=nam[:, 0, :],
                                       op0=ALU.add, op1=ALU.add)
                st.done(v.tensor_scalar(gidx[:, :], nam[:, 1, :], -1.0, 0.0, ALU.add, ALU.max))
                st.done(v.tensor_single_scalar(gidx[:, :], gidx[:, :], 1, ALU.logical_shift_right))
                dve.wait_ge(l.gates, 1)
                st.done(v.tensor_scalar(gate[:, :, :], gate[:, :, :], 0.5, None, ALU.mult))
                v.engine_nop().then_inc(l.routed, 1)

            def experts(l):
                def x_lo(s, b):
                    dve.wait_ge(l.x_hi, s + 1)
                    v.tensor_tensor(xT[1][:, b], ps[:, b, :].rearrange("p (u c t) -> p u c t", u=2, c=KC),
                                    xT[0][:, b].bitcast(F32), ALU.subtract).then_inc(l.x_lo, 1)

                def a_lo(s):
                    dve.wait_ge(l.a_hi, s + 1)
                    v.tensor_tensor(aT[1][:, :, :, :], ps[:, 6, :].rearrange("p (u c t) -> p u c t", u=2, c=KC),
                                    aT[0][:, :, :, :].bitcast(F32), ALU.subtract).then_inc(l.a_lo, 1)

                def activate(s, b):
                    for u in range(2):
                        dve.wait_ge(l.glu, s * 2 + u + 1)
                        ins = v.tensor_scalar(upv[:, u, :],
                                              ps[:, 2 + 2 * b + u, :].rearrange("p (f c) -> p f c", c=2)[:, :, 1],
                                              1.0 - LIMIT, 1.0 + LIMIT, ALU.max, ALU.min)
                    st.done(ins)
                    v.scalar_tensor_tensor(out=act_v[:, b], in0=glu[:, b], scalar=GLU_LIMIT, in1=upv[:, :, :],
                                           op0=ALU.min, op1=ALU.mult).then_inc(l.act, 1)

                x_lo(0, 0)
                x_lo(1, 1)
                activate(0, 0)

                def body(it):
                    for d in range(2):
                        s, b = it * 2 + 1 + d, (1 + d) % 2
                        x_lo(s + 1, 1 - b)
                        a_lo(s - 1)
                        activate(s, b)
                st.loop(NP // 2 - 1, 2, body)
                a_lo(NP - 2)
                activate(NP - 1, 1)
                a_lo(NP - 1)

            def combine(l, g, j, k):
                dve.wait_ge(l.y_loaded[j], 16 * (k + 1))
                for c in range(TOPK):
                    for u in range(2):
                        xr = xs[:, bass.ds(g * 2 + u, 1), :].rearrange("p a h -> p (a h)")
                        ins = v.scalar_tensor_tensor(out=xr, in0=ybuf[:, j, u, c, :],
                                                     scalar=gate[:, c, bass.ds(g * 2 + u, 1)], in1=xr,
                                                     op0=ALU.mult, op1=ALU.add)
                    if c == 0:
                        st.done(ins)
                ins.then_inc(l.y_used, 1)
                dve.wait_ge(l.y_used, g + 1)

            route(0)
            experts(L[0])

            def xT_low(g, b):
                dve.wait_ge(A.x_hi, g + 1)
                v.tensor_tensor(xT[1][:, b], ps[:, b, :].rearrange("p (u c t) -> p u c t", u=2, c=KC),
                                xT[0][:, b].bitcast(F32), ALU.subtract).then_inc(A.x_lo, 1)

            def rotate(g, b):
                dve.wait_ge(qk_sb, g + 1)
                wait(dve, rot_done, g)
                for u in range(2):
                    w = qk[:, b, u, :].rearrange("p (h j c) -> p h j c", j=HD // 2, c=2)
                    sin = cst[:, bass.ds(g * 2 * ROT + (C_SIN + u * ROT), ROT)][:, None, :].to_broadcast(
                        [P, 2 * HEADS, ROT])
                    v.tensor_tensor(rotr[:, u], w[:, :, 0:ROT, 1], sin, ALU.mult)
                    ins = v.tensor_tensor(roti[:, u], w[:, :, 0:ROT, 0], sin, ALU.mult)
                st.done(ins)
                for u in range(2):
                    w = qk[:, b, u, :].rearrange("p (h j c) -> p h j c", j=HD // 2, c=2)
                    ins = v.tensor_scalar(w[:, :, 0, :], w[:, :, 0, :], cst[:, bass.ds(g * 2 + (C_COS + u), 1)], None,
                                          ALU.mult)
                ins.then_inc(rot_parts, 1)

            def first_pass(g, j, it):
                b, static = j % 2, isinstance(g, int)
                wait(dve, g_used, g - 3)
                normalise(A, xn_a[:, j], g, b)
                if not (static and g < 2):
                    rotate(g - 2, b)
                if not (static and g == NG - 1):
                    combine(L[0], g + 1, (j + 1) % 4, it + (j + 1) // 4)
                    moments(A, g + 1, 1 - b)
                xT_low(g, b)

            combine(L[0], 0, 0, 0)
            v.memset(xn_a[:, :, :, H:H + 1], 1.0)
            v.memset(xn_a[:, :, :, H + 1:H + 2], 0.0)
            moments(A, 0, 0)
            st.stages(20, first_pass)
            rotate(NG - 2, 0)
            rotate(NG - 1, 1)

            dve.wait_ge(g_used, NG)
            v.tensor_copy(gsb, ps[:, 6:8, 0:H + 2]).then_inc(mid_dve, 1)
            dve.wait_ge(mid_pe, 1)
            v.tensor_copy(gT.rearrange("p c o -> p (c o)"), ps[:, 2, :])
            v.tensor_copy(ksT[0:1, :], ps[0:1, 3, 0:H]).then_inc(mid_dve, 1)
            dve.wait_ge(mid_pe, 3)
            v.tensor_tensor(sT, ps[:, 5, 0:KC * P].rearrange("p (a k) -> p a k", a=KC),
                            cst[:, None, C_BLK:C_BLK + P].to_broadcast([P, KC, P]), ALU.mult).then_inc(mid_dve, 1)
            dve.wait_ge(m_hi, 1)
            v.tensor_tensor(qk_w[1][:, :, 0:H], ps[:, 4, :].rearrange("p (a o) -> p a o", a=KC),
                            qk_w[0][:, :, 0:H].bitcast(F32), ALU.subtract).then_inc(m_lo, 1)
            dve.wait_ge(m_lo, 1)
            v.engine_nop().then_inc(mid_dve, 1)

            l1 = L[1]

            def q_low(g, b):
                dve.wait_ge(q_hi, g + 1)
                v.tensor_tensor(xT[1][:, b], ps[:, 2 + b, :].rearrange("p (u c t) -> p u c t", u=2, c=KC),
                                xT[0][:, b].bitcast(F32), ALU.subtract).then_inc(q_lo, 1)

            def add_out(g, b):
                dve.wait_ge(o_ps, g + 1)
                xr = pair(xs, g)
                v.tensor_tensor(xr, xr, ps[:, 4 + b, :].rearrange("p (u h) -> p u h", u=2), ALU.add).then_inc(x_done, 1)
                dve.wait_ge(x_done, g + 1)
                moments(l1, g, b)

            def second_pass(g, j, it):
                b, static = j % 2, isinstance(g, int)
                k = it * 2 + j // 2
                wait(dve, l1.xn_stored[b], 16 * k)
                normalise(l1, xn_r[:, b], g, b)
                if not (static and g + 1 >= NG):
                    add_out(g + 1, 1 - b)
                if not (static and g + 3 >= NG):
                    q_low(g + 3, 1 - b)

            q_low(0, 0)
            q_low(1, 1)
            add_out(0, 0)
            q_low(2, 0)
            st.stages(12, second_pass)
            route(1)
            experts(l1)

            def last_body(it):
                for j in range(4):
                    combine(l1, it * 4 + j, j, it)
            st.loop(NG // 4, 4, last_body)


_INS = ["L0_attn_x", "L0_attn_Wq", "L0_attn_bq", "L0_attn_Wk", "L0_attn_bk", "L0_attn_Wv", "L0_attn_bv",
        "L0_attn_Wo", "L0_attn_bo", "L0_ffn_router_weight", "L0_ffn_gate_up_proj", "L0_ffn_gate_up_proj_bias",
        "L0_ffn_down_proj", "L0_ffn_down_proj_bias"]


def constants():
    import numpy as np
    c = np.zeros((P, NCONST), np.float32)
    c[:, C_ID:C_ID + P] = np.eye(P)
    c[:, C_UP:C_UP + P] = np.triu(np.ones((P, P)), 1)
    c[:, C_BLK:C_BLK + P] = np.kron(np.eye(P // HD), np.ones((HD, HD))) / np.sqrt(HD)
    freqs = np.zeros(ROT, np.float32)
    for j in range(ROT):
        freqs[j] = np.float32(1.0) / np.float32(10000.0 ** (2 * j))
    angles = np.arange(T, dtype=np.float32)[:, None] * freqs[None, :]
    c[:, C_COS:C_COS + NT] = np.cos(angles[:, 0]).reshape(P, NT)
    c[:, C_SIN:C_SIN + NT * ROT] = np.sin(angles).reshape(P, NT * ROT)
    c[:, C_P] = np.arange(P)
    c[:, C_E:C_E + E] = np.arange(E)
    return c


def kernel(**inputs):
    import numpy as np
    import concourse.bacc as bacc
    from concourse.bass_utils import run_bass_kernel_spmd

    nc = bacc.Bacc("TRN2", target_bir_lowering=False, num_devices=1)
    arrays = {name: np.ascontiguousarray(inputs[name]) for name in _INS}
    arrays["constants"] = constants()
    args = [nc.dram_tensor(name, a.shape, mybir.dt.from_np(a.dtype), kind="ExternalInput").ap()
            for name, a in arrays.items()]
    out = nc.dram_tensor("out", (1, T, H), F32, kind="ExternalOutput").ap()
    build(nc, *args, out)
    r = run_bass_kernel_spmd(nc, [arrays], core_ids=[0])
    return r.results[0]["out"]
```

```python
from contextlib import ExitStack

import concourse.bass as bass
from concourse import mybir

ALU = mybir.AluOpType
ACT = mybir.ActivationFunctionType
AX = mybir.AxisListType
F32 = mybir.dt.float32
F32R = mybir.dt.float32r
BF16 = mybir.dt.bfloat16
I32 = mybir.dt.int32
U32 = mybir.dt.uint32

P = 128
T, H = 4096, 256
NT = T // P
NG = NT // 2
KC = H // P
E, I = 8, 256
F = 2 * I
TOPK = 2
HEADS, HD = 16, 16
ROT = 5
NQ = TOPK * NT
NS = T * TOPK // P + E
NP = NS // 2
QC = 8
NQC = NQ // QC
PAD = 16
LIMIT, ALPHA = 7.0, 1.702
EPS = 1e-5
GLU_LIMIT = 6.9999536
MASKED = -3.0e38
SKIP = 16384.0

C_ID, C_UP, C_BLK = 0, P, 2 * P
C_COS = 3 * P
C_SIN = C_COS + NT
C_P = C_SIN + NT * ROT
C_EPS = C_P + 2
C_E = C_EPS + 1
NCONST = C_E + E

B_UP, B_DN = 0, E * F
B_QK = B_DN + E * H
B_O = B_QK + 2 * H
NB = B_O + H

WORK = 8192


def wait(eng, sem, n):
    if not (isinstance(n, int) and n <= 0):
        eng.wait_ge(sem, n)


def repeat(eng, count, body):
    body(0)
    with eng.Fori(1, count) as it:
        body(it)


def stages(eng, step):
    for g in range(4):
        step(g, g, 0)
    with eng.Fori(1, NG // 4 - 1) as it:
        for j in range(4):
            step(it * 4 + j, j, it)
    for g in range(NG - 4, NG):
        step(g, g % 4, g // 4)


class Steps:

    def __init__(self, eng, sem, passed):
        self.eng, self.sem, self.passed, self.n, self.done_in_body = eng, sem, passed, 0, 0

    def hold(self):
        self.eng.sem_inc(self.passed, 1)

    def mark(self, ins):
        self.n = self.n + 1
        self.done_in_body += 1
        ins.then_inc(self.sem, 1)
        return self.n

    def need(self, n):
        self.eng.wait_ge(self.sem, n)

    def done(self, ins):
        self.need(self.mark(ins))

    def stages(self, per, step):
        for g in range(4):
            step(g, g, 0)
        base = self.n
        with self.eng.Fori(1, NG // 4 - 1) as it:
            self.n, self.done_in_body = base + (it - 1) * per, 0
            for j in range(4):
                step(it * 4 + j, j, it)
            assert self.done_in_body == per, self.done_in_body
        self.n = base + (NG // 4 - 2) * per
        for g in range(NG - 4, NG):
            step(g, g % 4, g // 4)

    def loop(self, count, per, body):
        base = self.n
        body(0)
        with self.eng.Fori(1, count) as it:
            self.n, self.done_in_body = base + it * per, 0
            body(it)
            assert self.done_in_body == per, self.done_in_body
        self.n = base + count * per


def build(nc, x, Wq, bq, Wk, bk, Wv, bv, Wo, bo, Wr, Wup, bup, Wdn, bdn, consts, out):
    ctx = ExitStack()

    def sb(name, shape, dt):
        return ctx.enter_context(nc.sbuf_tensor(name, shape, dt))

    def sem(name):
        return ctx.enter_context(nc.semaphore(name))

    def scratch(name, shape, dt=F32):
        return nc.dram_tensor(name, shape, dt).ap()

    with ctx:
        xn_dram = [scratch(f"xn_dram{n}", [T, H]) for n in range(2)]
        y_dram = [scratch(f"y_dram{n}", [T * TOPK, H]) for n in range(2)]
        q_dram = scratch("q_dram", [P, NT, H])
        bias_dram = scratch("bias_dram", [3, NB], BF16)

        xs = sb("xs", [P, NT, H], F32)
        up_w = [sb(f"up_{h}", [P, KC, E, F], F32R) for h in ("hi", "lo")]
        dn_w = [sb(f"dn_{h}", [P, KC, E, H], F32R) for h in ("hi", "lo")]
        qk_w = [sb(f"qk_{h}", [P, KC, 2 * H], F32R) for h in ("hi", "lo")]
        wr = sb("wr", [P, KC, E], F32)
        biases = sb("biases", [P, NB], BF16)
        xT = [sb(f"xT_{h}", [P, 2, 2, KC, P], F32R) for h in ("hi", "lo")]
        aT = [sb(f"aT_{h}", [P, 2, KC, P], F32R) for h in ("hi", "lo")]
        xn1 = [sb(f"xn1_{h}", [P, 2, 2, H + 2], F32R) for h in ("hi", "lo")]
        cst = sb("cst", [P, NCONST], F32)
        ones = sb("ones", [P, P], BF16)
        numbers = sb("numbers", [P, 4 * QC], BF16)
        upper = sb("upper", [P, P], BF16)
        logit = sb("logit", [P, NT, E], F32)
        gate = sb("gate", [P, TOPK, NT], F32)
        gidx = sb("gidx", [P, NS], U32)
        sidx = sb("sidx", [P, NS], U32)
        gslot = sb("gslot", [P, 2, 2], U32)
        sslot = sb("sslot", [P, 2, 2], U32)
        expert = sb("expert", [1, NS], I32)
        small = sb("small", [P, 48], F32)
        bst = sb("bst", [P, 2, 6], F32)
        sbmv = sb("sbmv", [P, 8], F32)
        work = sb("work", [P, WORK], F32)
        ps = ctx.enter_context(nc.psum_tensor("ps", [P, 8, 512], F32))

        ident = cst[:, C_ID:C_ID + P]

        def area(at, *shape, dt=F32):
            n = 1
            for d in shape:
                n *= d
            words = n // 2 if dt is BF16 else n
            assert at + words <= WORK
            v = work[:, at:at + words]
            if dt is not F32:
                v = v.bitcast(dt)
            names = "abcd"[:len(shape)]
            if len(shape) == 1:
                return v
            return v.rearrange(f"p ({' '.join(names)}) -> p {' '.join(names)}",
                               **dict(zip(names[1:], shape[1:])))

        raw = area(3136, 2, 1536)
        iotaS = area(2048, P, QC, dt=BF16)
        iotaJ = area(2560, NS, QC, dt=BF16)
        xn_r = area(0, 2, 2, H)
        xTf = area(1024, 2, 2, KC, P)
        xg = area(0, 2, 2, H)
        glu = area(1024, 2, 2, I)
        upv = area(2048, 2, I)
        act_v = area(2560, 2, 2, I)
        ysb = area(3584, 2, 2, H)
        ybuf = area(0, 4, 2, TOPK, H)
        xn_a = area(2048, 4, 2, H)
        qk = area(4096, 2, 2, 2 * H)
        rotr = area(6144, 2, 2 * HEADS, ROT)
        roti = area(6464, 2, 2 * HEADS, ROT)
        wv = area(6784, KC, H)
        wo = area(7296, KC, H)
        bvrow = area(7808, H)
        gsb = area(0, KC, H + 2)
        gT = area(516, KC, H)
        ksT = area(1028, H)
        sT = area(1284, KC, P)
        qin = area(3136, 4, 2, H)
        bstage = area(6208, 54)
        bparts = area(6272, 3, 54, dt=BF16)
        bres = area(6400, 54)
        iint = area(6464, 2 * 576, dt=I32)

        x_loaded = [sem(f"x_loaded{c}") for c in range(4)]
        consts_loaded = sem("consts_loaded")
        router_loaded = sem("router_loaded")
        out_w_loaded = sem("out_w_loaded")
        raw_loaded = [sem(f"raw_loaded{b}") for b in range(2)]
        raw_hi = sem("raw_hi")
        raw_lo = sem("raw_lo")
        bias_loaded = sem("bias_loaded")
        bias_split = sem("bias_split")
        bias_stored = sem("bias_stored")
        bias_ready = sem("bias_ready")
        bias_zeroed = sem("bias_zeroed")
        consts_made = sem("consts_made")
        iotas_made = sem("iotas_made")
        dve_step = sem("dve_step")
        pool_step = sem("pool_step")
        pool_passed = sem("pool_passed")
        dve_passed = sem("dve_passed")

        class Norm:

            def __init__(self, n):
                s = self.s = lambda name: sem(f"{name}{n}")
                self.var, self.sd, self.xn = s("var"), s("sd"), s("xn")
                self.x_T, self.x_hi, self.x_lo = s("x_T"), s("x_hi"), s("x_lo")

        class Layer(Norm):

            def __init__(self, n):
                super().__init__(n)
                s = self.s
                self.xn_stored = [s("xn_stored_a"), s("xn_stored_b")]
                self.xn_T, self.xn_Tsb = s("xn_T"), s("xn_Tsb")
                self.logits, self.logit_sb = s("logits"), s("logit_sb")
                self.mask, self.prefix, self.gap, self.gates = s("mask"), s("prefix"), s("gap"), s("gates")
                self.hot_tile, self.hot, self.hot_hi = s("hot_tile"), s("hot"), s("hot_hi")
                self.hot_used, self.routed = s("hot_used"), s("routed")
                self.gathered = [s("gathered_a"), s("gathered_b")]
                self.scattered = [s("scattered_a"), s("scattered_b")]
                self.gu, self.glu, self.act = s("gu"), s("glu"), s("act")
                self.a_T, self.a_hi, self.a_lo = s("a_T"), s("a_hi"), s("a_lo")
                self.y_ps, self.y_sb = s("y_ps"), s("y_sb")
                self.y_loaded = [s(f"y_loaded_{j}") for j in range(4 if n else 2)]
                self.y_used = s("y_used")

        L = [Layer(0), Layer(1)]
        A = Norm(2)
        qk_ps, qk_sb, rot_parts, rot_done = sem("qk_ps"), sem("qk_sb"), sem("rot_parts"), sem("rot_done")
        xn_hi, xn_lo, rot_cos = sem("xn_hi"), sem("xn_lo"), sem("rot_cos")
        k_hi, k_lo, g_used = sem("k_hi"), sem("k_lo"), sem("g_used")
        q_stored = [sem("q_stored_a"), sem("q_stored_b")]
        q_loaded = [sem(f"q_loaded_{j}") for j in range(4)]
        mid_pe, mid_dve, m_hi, m_lo = sem("mid_pe"), sem("mid_dve"), sem("m_hi"), sem("m_lo")
        q_T, q_hi, q_lo, o_ps, x_done = sem("q_T"), sem("q_hi"), sem("q_lo"), sem("o_ps"), sem("x_done")
        out_stored = sem("out_stored")

        block = ctx.enter_context(nc.Block())
        x_v = x.rearrange("b (p i) h -> p (b i) h", p=P)
        out_v = out.rearrange("b (p i) h -> p (b i) h", p=P)
        xn_v = [d.rearrange("(p i) h -> p i h", p=P) for d in xn_dram]
        y_v = [d.rearrange("(p i k) h -> p i k h", p=P, k=TOPK) for d in y_dram]

        def pair(v, g):
            return v[:, bass.ds(g * 2, 2)]

        def hot(b):
            at = 3136 + b * 1376
            return (area(at, P, QC, dt=BF16),) + tuple(area(at + 512 + 288 * n, NS, QC, dt=BF16) for n in range(3))

        @block.sync
        def _(sp):
            sp.dma_start(cst[:, :], consts).then_inc(consts_loaded, 16)

            def load_x(c):
                sp.dma_start(xs[:, 8 * c:8 * c + 8, :], x_v[:, 8 * c:8 * c + 8, :]).then_inc(x_loaded[c], 16)

            load_x(0)
            load_x(1)

            def load_raw(e, b):
                sp.dma_start(raw[:, b, 0:KC * F].rearrange("p (c f) -> p c f", c=KC),
                             Wup[bass.ds(e, 1)].rearrange("a (c p) f -> p (a c) f", p=P)).then_inc(raw_loaded[b], 16)
                sp.dma_start(raw[:, b, KC * F:KC * (F + H)].rearrange("p (c f) -> p c f", c=KC),
                             Wdn[bass.ds(e, 1)].rearrange("a (c p) f -> p (a c) f", p=P)).then_inc(raw_loaded[b], 16)

            load_raw(0, 0)

            def store_xn(g, j, it):
                static = isinstance(g, int)
                sp.wait_ge(L[0].xn, g + 1)
                sp.dma_start(pair(xn_v[0], g), xn_r[:, j % 2]).then_inc(L[0].xn_stored[j % 2], 16)
                if static and g == 0:
                    load_raw(1, 1)
                if static and g in (1, 2):
                    load_x(g + 1)
                if static and g == 3:
                    sp.wait_ge(bias_split, 1)
                    for at, n, col in ((0, 32, B_UP), (32, 16, B_DN), (48, 2, B_QK), (50, 2, B_QK + H), (52, 2, B_O)):
                        sp.dma_start(bias_dram[:, col:col + P * n].rearrange("k (p c) -> p k c", p=P),
                                     bparts[:, :, at:at + n]).then_inc(bias_stored, 16)
                if static and g == NG - 1:
                    sp.wait_ge(raw_lo, E - 1)
                    for w, c in ((Wq, 0), (Wk, H)):
                        sp.dma_start(raw[:, 0, 0:KC * 2 * H].rearrange("p (c f) -> p c f", c=KC)[:, :, c:c + H],
                                     w.rearrange("(c p) f -> p c f", p=P)).then_inc(raw_loaded[0], 16)
                elif j % 2 and not (static and g == 1):
                    e, b = it * 2 + (j + 1) // 2, (j + 1) // 2 % 2
                    sp.wait_ge(raw_lo, e - 1)
                    load_raw(e, b)
            stages(sp, store_xn)
            sp.wait_ge(bias_stored, 16 * 5)
            sp.wait_ge(bias_zeroed, 1)
            sp.dma_start(biases[0:3, :], bias_dram[:, :]).then_inc(bias_ready, 16)

            def wait_scattered(n):
                for b in range(2):
                    sp.wait_ge(L[n].scattered[b], 32 * (NP // 2))

            wait_scattered(0)
            for b in range(2):
                sp.dma_start(ybuf[:, b], pair(y_v[0], b)).then_inc(L[0].y_loaded[b], 16)
            sp.dma_start(wv, Wv.rearrange("(c p) o -> p c o", p=P)).then_inc(out_w_loaded, 16)
            sp.dma_start(wo, Wo.rearrange("(c p) o -> p c o", p=P)).then_inc(out_w_loaded, 16)
            sp.dma_start(bvrow[0:1, :], bv.rearrange("(a o) -> a o", a=1)).then_inc(out_w_loaded, 16)
            with sp.Fori(0, NG // 2 - 1) as it:
                for b in range(2):
                    g = it * 2 + b
                    sp.wait_ge(L[0].y_used, g + 1)
                    sp.dma_start(ybuf[:, b], pair(y_v[0], g + 2)).then_inc(L[0].y_loaded[b], 16)

            for b in range(2):
                sp.wait_ge(q_stored[b], 16 * (NG // 2))
            sp.wait_ge(g_used, NG)
            for j in range(4):
                sp.dma_start(qin[:, j], pair(q_dram, j)).then_inc(q_loaded[j], 16)
            with sp.Fori(0, NG // 4 - 1) as it:
                for j in range(4):
                    g = it * 4 + j
                    sp.wait_ge(q_T, g + 1)
                    sp.dma_start(qin[:, j], pair(q_dram, g + 4)).then_inc(q_loaded[j], 16)

            wait_scattered(1)
            for j in range(4):
                sp.dma_start(ybuf[:, j], pair(y_v[1], j)).then_inc(L[1].y_loaded[j], 16)

            def finish(g, j, more):
                sp.wait_ge(L[1].y_used, g + 1)
                if more:
                    sp.dma_start(ybuf[:, j], pair(y_v[1], g + 4)).then_inc(L[1].y_loaded[j], 16)
                sp.dma_start(pair(out_v, g), pair(xs, g)).then_inc(out_stored, 16)

            with sp.Fori(0, NG // 4 - 1) as it:
                for j in range(4):
                    finish(it * 4 + j, j, True)
            for j in range(4):
                finish(NG - 4 + j, j, False)
            sp.wait_ge(out_stored, 16 * NG)

        @block.gpsimd
        def _(pool):
            st = Steps(pool, pool_step, pool_passed)
            pool.dma_start(wr[:, :, :], Wr.rearrange("(c p) e -> p c e", p=P)).then_inc(router_loaded, 16)

            numbers_v = numbers[:, :].rearrange("p (n k) -> p n k", k=QC)

            def make_iotas():
                for k, (dst, n, pattern, base) in enumerate((
                        (iotaS, P, [[1, P // 2], [0, QC]], 0),
                        (iotaS, P, [[1, P // 2], [0, QC]], P // 2),
                        (iotaJ, NS, [[1, NS], [0, QC]], 0),
                        (numbers_v, 4, [[QC, 4], [1, QC]], 1))):
                    n2 = pattern[0][1]
                    st.done(nc.gpsimd.iota(iint[:, 0:n2 * QC], pattern=pattern, base=base, channel_multiplier=0))
                    d = dst[:, base:base + n2, :] if n == P else dst[:, :, :]
                    st.done(nc.gpsimd.tensor_copy(d, iint[:, 0:n2 * QC].rearrange("p (a b) -> p a b", b=QC)))

            make_iotas()
            nc.gpsimd.memset(biases[:, :], 0.0).then_inc(bias_zeroed, 1)
            pool.sem_inc(iotas_made, 1)

            def low(c, b, parts):
                pool.wait_ge(raw_hi, c + 1)
                for j, (dst, src, hi) in enumerate(parts):
                    ins = nc.gpsimd.tensor_tensor(dst, src, hi.bitcast(F32), ALU.subtract)
                ins.then_inc(raw_lo, 1)

            def expert_parts(e, b, h):
                u, d = raw[:, b, 0:KC * F], raw[:, b, KC * F:KC * (F + H)]
                return ((up_w[h][:, :, bass.ds(e, 1), :].rearrange("p c a f -> p c (a f)"),
                         u.rearrange("p (c f) -> p c f", c=KC)),
                        (dn_w[h][:, :, bass.ds(e, 1), :].rearrange("p c a f -> p c (a f)"),
                         d.rearrange("p (c f) -> p c f", c=KC)))

            def body(it):
                for b in range(2):
                    e = it * 2 + b
                    low(e, b, [(lo, src, hi) for (lo, src), (hi, _) in
                               zip(expert_parts(e, b, 1), expert_parts(e, b, 0))])
            repeat(pool, E // 2, body)
            low(E, 0, [(qk_w[1][:, :, :], raw[:, 0, 0:KC * 2 * H].rearrange("p (c f) -> p c f", c=KC),
                        qk_w[0][:, :, :])])

            def experts(n):
                l = L[n]
                for b in range(2):
                    pool.wait_ge(l.xn_stored[b], 16 * (NG // 2))
                pool.wait_ge(l.routed, 1)

                def gather(s, b):
                    st.hold()
                    st.done(nc.gpsimd.tensor_copy(gslot[:, b, :], gidx[:, bass.ds(s * 2, 2)]))
                    st.hold()
                    for u in range(2):
                        pool.indirect_dma_start(xg[:, b, u, :], None, xn_dram[n],
                                                bass.IndirectOffsetOnAxis(ap=gslot[:, b, u:u + 1], axis=0)
                                                ).then_inc(l.gathered[b], 16)

                def scatter(s, b, k):
                    pool.wait_ge(l.y_sb, s + 1)
                    wait(pool, l.scattered[b], 32 * k)
                    st.hold()
                    st.done(nc.gpsimd.tensor_copy(sslot[:, b, :], sidx[:, bass.ds(s * 2, 2)]))
                    st.hold()
                    for u in range(2):
                        pool.indirect_dma_start(y_dram[n], bass.IndirectOffsetOnAxis(ap=sslot[:, b, u:u + 1], axis=0),
                                                ysb[:, b, u, :], None, bounds_check=T * TOPK - 1,
                                                oob_is_err=False).then_inc(l.scattered[b], 16)

                for s in range(2):
                    gather(s, s)
                for s in range(2, 6):
                    pool.wait_ge(l.x_T, s - 1)
                    gather(s, s % 2)

                def body(it):
                    for b in range(2):
                        s = it * 2 + b
                        scatter(s, b, it)
                        pool.wait_ge(l.x_T, s + 5)
                        gather(s + 6, b)
                st.loop((NP - 6) // 2, 4, body)
                for s in range(NP - 6, NP):
                    scatter(s, s % 2, s // 2)

            experts(0)

            def first_pass(g, j, it):
                b = j % 2
                pool.wait_ge(xn_hi, g + 1)
                nc.gpsimd.tensor_tensor(xn1[1][:, b, :, 0:H], xn_a[:, j],
                                        xn1[0][:, b, :, 0:H].bitcast(F32), ALU.subtract).then_inc(xn_lo, 1)
                v = qk[:, b].rearrange("p u (h j c) -> p u h j c", j=HD // 2, c=2)
                pool.wait_ge(rot_cos, g + 1)
                r, i = v[:, :, :, 0:ROT, 0], v[:, :, :, 0:ROT, 1]
                for u in range(2):
                    nc.gpsimd.tensor_tensor(r[:, u], r[:, u], rotr[:, u], ALU.subtract)
                for u in range(2):
                    ins = nc.gpsimd.tensor_tensor(i[:, u], i[:, u], roti[:, u], ALU.add)
                ins.then_inc(rot_done, 1)
                pool.wait_ge(k_hi, g + 1)
                nc.gpsimd.tensor_tensor(aT[1].rearrange("p u c k -> p u (c k)"), qk[:, b, :, H:2 * H],
                                        aT[0].rearrange("p u c k -> p u (c k)").bitcast(F32),
                                        ALU.subtract).then_inc(k_lo, 1)

            stages(pool, first_pass)
            pool.wait_ge(mid_dve, 4)
            for b in range(2):
                pool.wait_ge(q_stored[b], 16 * (NG // 2))
            make_iotas()
            pool.sem_inc(iotas_made, 1)
            experts(1)

        @block.scalar
        def _(act):
            segs = ((bup.rearrange("e f -> (e f)"), 0, 32), (bdn.rearrange("e f -> (e f)"), 32, 16),
                    (bq, 48, 2), (bk, 50, 2), (bo, 52, 2))
            for src, at, n in segs:
                act.dma_start(bstage[:, at:at + n], src.rearrange("(p c) -> p c", p=P)).then_inc(bias_loaded, 16)

            def high_up(e, b, k):
                act.wait_ge(raw_loaded[b], 32 * (k + 1))
                nc.scalar.activation(up_w[0][:, :, bass.ds(e, 1), :].rearrange("p c a f -> p c (a f)"),
                                     raw[:, b, 0:KC * F].rearrange("p (c f) -> p c f", c=KC), ACT.Copy)

            def high_down(e, b):
                nc.scalar.activation(dn_w[0][:, :, bass.ds(e, 1), :].rearrange("p c a f -> p c (a f)"),
                                     raw[:, b, KC * F:KC * (F + H)].rearrange("p (c f) -> p c f", c=KC),
                                     ACT.Copy).then_inc(raw_hi, 1)

            def sqrt_var(l, b, g):
                act.wait_ge(l.var, g + 1)
                nc.scalar.activation(small[:, 8 + 2 * b:10 + 2 * b],
                                     sbmv[:, 4 * b:4 * b + 4].rearrange("p (u c) -> p u c", c=2)[:, :, 1],
                                     ACT.Sqrt, bias=cst[:, C_EPS:C_EPS + 1]).then_inc(l.sd, 1)

            def xn_out(l, n, g, b):
                act.wait_ge(l.xn_T, g + 1)
                if n == 1:
                    act.dma_start(pair(xn_v[n], g), xn_r[:, b]).then_inc(l.xn_stored[b], 16)
                nc.scalar.activation(xTf[:, b], ps[:, b, :].rearrange("p (u c t) -> p u c t", u=2, c=KC),
                                     ACT.Copy).then_inc(l.xn_Tsb, 1)

            def logits_out(l, g, b):
                act.wait_ge(l.logits, g + 1)
                nc.scalar.activation(pair(logit, g), ps[:, 6 + b, 0:2 * E].rearrange("p (u e) -> p u e", u=2),
                                     ACT.Copy).then_inc(l.logit_sb, 1)

            def norm_step(l, n, g, b, first=False, last=False, down=None):
                if not last:
                    sqrt_var(l, 1 - b, g + 1)
                if down is not None:
                    down()
                xn_out(l, n, g, b)
                if not first:
                    logits_out(l, g - 1, 1 - b)

            sqrt_var(L[0], 0, 0)

            def first_norm(g, j, it):
                static = isinstance(g, int)
                down = None
                if j % 2 == 0 and not (static and g == 0):
                    down = lambda: high_down(it * 2 + j // 2 - 1, 1 - j // 2)
                norm_step(L[0], 0, g, j % 2, first=static and g == 0, last=static and g == NG - 1, down=down)
                if j % 2:
                    high_up(it * 2 + j // 2, j // 2, it)
            stages(act, first_norm)
            high_down(E - 1, 1)
            logits_out(L[0], NG - 1, 1)
            act.wait_ge(raw_loaded[0], 32 * (E // 2 + 1))
            nc.scalar.activation(qk_w[0][:, :, :], raw[:, 0, 0:KC * 2 * H].rearrange("p (c f) -> p c f", c=KC),
                                 ACT.Copy).then_inc(raw_hi, 1)

            def gates(l):
                act.wait_ge(l.gap, 1)
                nc.scalar.activation(gate[:, 1, :], small[:, 16:16 + NT], ACT.Sigmoid)
                nc.scalar.activation(gate[:, 0, :], small[:, 16:16 + NT], ACT.Sigmoid, scale=-1.0).then_inc(l.gates, 1)
                for ch in range(NQC):
                    act.wait_ge(l.hot_tile, ch + 1)
                    if ch >= 2:
                        act.wait_ge(l.hot_used, ch - 1)
                    _, ht, _, high = hot(ch % 2)
                    half = C_P + ch // (NQC // 2)
                    nc.scalar.activation(high, ht, ACT.Copy, scale=cst[:, half:half + 1]).then_inc(l.hot_hi, 1)

            def experts(l):
                def x_hi(s, b):
                    act.wait_ge(l.x_T, s + 1)
                    nc.scalar.activation(xT[0][:, b], ps[:, b, :].rearrange("p (u c t) -> p u c t", u=2, c=KC),
                                         ACT.Copy).then_inc(l.x_hi, 1)

                def a_hi(s):
                    act.wait_ge(l.a_T, s + 1)
                    nc.scalar.activation(aT[0][:, :, :, :], ps[:, 6, :].rearrange("p (u c t) -> p u c t", u=2, c=KC),
                                         ACT.Copy).then_inc(l.a_hi, 1)

                def glus(s, b):
                    wait(act, l.act, s - 1)
                    for u in range(2):
                        act.wait_ge(l.gu, s * 2 + u + 1)
                        nc.scalar.activation(glu[:, b, u, :],
                                             ps[:, 2 + 2 * b + u, :].rearrange("p (f c) -> p f c", c=2)[:, :, 0],
                                             ACT.Gelu_apprx_sigmoid).then_inc(l.glu, 1)

                def y_out(s, b, k):
                    act.wait_ge(l.y_ps, s + 1)
                    wait(act, l.scattered[b], 32 * k)
                    nc.scalar.activation(ysb[:, b], ps[:, 7, :].rearrange("p (u h) -> p u h", u=2),
                                         ACT.Copy).then_inc(l.y_sb, 1)

                x_hi(0, 0)
                x_hi(1, 1)
                glus(0, 0)
                def body(it):
                    for d in range(2):
                        s, b = it * 2 + 1 + d, (1 + d) % 2
                        x_hi(s + 1, 1 - b)
                        a_hi(s - 1)
                        glus(s, b)
                        y_out(s - 1, 1 - b, it)
                repeat(act, NP // 2 - 1, body)
                a_hi(NP - 2)
                glus(NP - 1, 1)
                y_out(NP - 2, 0, NP // 2 - 1)
                a_hi(NP - 1)
                y_out(NP - 1, 1, NP // 2 - 1)

            gates(L[0])
            experts(L[0])

            def xT_high(g, b):
                act.wait_ge(A.x_T, g + 1)
                nc.scalar.activation(xT[0][:, b], ps[:, b, :].rearrange("p (u c t) -> p u c t", u=2, c=KC),
                                     ACT.Copy).then_inc(A.x_hi, 1)

            def qk_out(g, b, k):
                wait(act, q_stored[b], 16 * k)
                wait(act, k_lo, g - 1)
                for u in range(2):
                    act.wait_ge(qk_ps, g * 2 + u + 1)
                    ins = nc.scalar.activation(qk[:, b, u, :], ps[:, 2 + 2 * b + u, :], ACT.Copy)
                ins.then_inc(qk_sb, 1)

            def xn_high(g, j):
                wait(act, g_used, g - 1)
                nc.scalar.activation(xn1[0][:, j % 2, :, 0:H], xn_a[:, j], ACT.Copy).then_inc(xn_hi, 1)

            def scale_cos(g, b):
                act.wait_ge(rot_parts, g + 1)
                for u in range(2):
                    w = qk[:, b, u, :].rearrange("p (h j c) -> p h j c", j=HD // 2, c=2)
                    ins = nc.scalar.activation(w[:, :, 0, :], w[:, :, 0, :], ACT.Copy,
                                               scale=cst[:, bass.ds(g * 2 + (C_COS + u), 1)])
                ins.then_inc(rot_cos, 1)

            def store_q(g, b):
                act.dma_start(pair(q_dram, g), qk[:, b, :, 0:H]).then_inc(q_stored[b], 16)

            def k_high(g, b):
                act.wait_ge(rot_done, g + 1)
                wait(act, g_used, g)
                nc.scalar.activation(aT[0].rearrange("p u c k -> p u (c k)"), qk[:, b, :, H:2 * H],
                                     ACT.Copy).then_inc(k_hi, 1)

            def first_pass(g, j, it):
                b, static = j % 2, isinstance(g, int)
                if not (static and g < 2):
                    xn_high(g - 2, (j + 2) % 4)
                    scale_cos(g - 2, b)
                if not (static and not 1 <= g <= NG):
                    qk_out(g - 1, 1 - b, it * 2 + (j - 1) // 2)
                if not (static and g >= NG):
                    xT_high(g, b)
                if not (static and g >= NG - 1):
                    sqrt_var(A, 1 - b, g + 1)
                if not (static and g < 2):
                    k_high(g - 2, b)
                    store_q(g - 2, b)

            sqrt_var(A, 0, 0)
            stages(act, first_pass)
            for g in range(NG, NG + 2):
                first_pass(g, g % 4, g // 4)

            def q_high(g, b):
                act.wait_ge(q_T, g + 1)
                nc.scalar.activation(xT[0][:, b], ps[:, 2 + b, :].rearrange("p (u c t) -> p u c t", u=2, c=KC),
                                     ACT.Copy).then_inc(q_hi, 1)

            q_high(0, 0)
            q_high(1, 1)
            act.wait_ge(mid_pe, 4)
            nc.scalar.activation(qk_w[0][:, :, 0:H], ps[:, 4, :].rearrange("p (a o) -> p a o", a=KC),
                                 ACT.Copy).then_inc(m_hi, 1)
            q_high(2, 0)
            sqrt_var(L[1], 0, 0)

            def second_pass(g, j, it):
                b = j % 2
                static = isinstance(g, int)
                if not (static and g + 3 >= NG):
                    q_high(g + 3, 1 - b)
                norm_step(L[1], 1, g, b, first=static and g == 0, last=static and g == NG - 1)
            stages(act, second_pass)
            logits_out(L[1], NG - 1, 1)
            gates(L[1])
            experts(L[1])

        @block.tensor
        def _(pe):
            def transpose4(bank, src):
                for u in range(2):
                    for c in range(KC):
                        k = (u * KC + c) * P
                        ins = nc.tensor.transpose(ps[:, bank, k:k + P], src[:, u, c * P:(c + 1) * P], ident)
                return ins

            def bias(out, at, width, start=True):
                nc.tensor.matmul(out, ones[:, :], biases[:, bass.ds(at, width)], start=True, stop=False)

            def product(out, st_hi, st_lo, mv_hi, mv_lo, stop):
                nc.tensor.matmul(out, st_hi, mv_hi, start=False, stop=False)
                nc.tensor.matmul(out, st_hi, mv_lo, start=False, stop=False)
                return nc.tensor.matmul(out, st_lo, mv_hi, start=False, stop=stop)

            pe.wait_ge(consts_loaded, 16)
            pe.wait_ge(consts_made, 1)
            pe.wait_ge(router_loaded, 16)

            def xn_transpose(l, g, b):
                pe.wait_ge(l.xn, g + 1)
                transpose4(b, xn_r[:, b]).then_inc(l.xn_T, 1)

            def logits(l, g, b):
                pe.wait_ge(l.xn_Tsb, g + 1)
                for u in range(2):
                    for c in range(KC):
                        ins = nc.tensor.matmul(ps[:, 6 + b, u * E:(u + 1) * E], xTf[:, b, u, c, :],
                                               wr[:, c, :], start=(c == 0), stop=(c == KC - 1))
                ins.then_inc(l.logits, 1)

            def layer_norm_loop(l):
                xn_transpose(l, 0, 0)
                def body(it):
                    for b in range(2):
                        g = it * 2 + b
                        xn_transpose(l, g + 1, 1 - b)
                        logits(l, g, b)
                repeat(pe, NG // 2 - 1, body)
                xn_transpose(l, NG - 1, 1)
                logits(l, NG - 2, 0)
                logits(l, NG - 1, 1)

            def route(l):
                pe.wait_ge(l.mask, 1)
                m = area(0, 256, dt=BF16)
                nc.tensor.matmul(ps[:, 2, 0:NT * E], upper[:, :], m, start=True, stop=True)
                nc.tensor.matmul(ps[:, 2, NT * E:2 * NT * E], ones[:, :], m, start=True, stop=True).then_inc(l.prefix, 1)
                for c in range(NQC):
                    pe.wait_ge(l.hot, c + 1)
                    pe.wait_ge(l.hot_hi, c + 1)
                    hs, _, low, high = hot(c % 2)
                    for k in range(QC):
                        first, last = c == 0 and k == 0, c == NQC - 1 and k == QC - 1
                        nc.tensor.matmul(ps[:, 3, 0:NS], hs[:, :, k], low[:, :, k], start=first, stop=last)
                        ins = nc.tensor.matmul(ps[:, 4, 0:NS], hs[:, :, k], high[:, :, k], start=first, stop=last)
                    ins.then_inc(l.hot_used, 1)

            names = [[pe.alloc_register(f"expert_{b}{u}") for u in range(2)] for b in range(2)]

            def experts(l):
                pe.wait_ge(l.routed, 1)
                pe.wait_ge(raw_lo, E + 1)
                pe.wait_ge(raw_hi, E + 1)
                pe.wait_ge(bias_ready, 16)

                def load_names(s, b):
                    pe.load(names[b], expert[0:1, bass.ds(s * 2, 2)])

                def named(b):
                    return [pe.snap(r, min_val=0, max_val=E - 1) for r in names[b]]

                def x_transpose(s, b, k):
                    pe.wait_ge(l.gathered[b], 32 * (k + 1))
                    transpose4(b, xg[:, b]).then_inc(l.x_T, 1)

                def up(s, b, u, e):
                    if u == 0:
                        pe.wait_ge(l.x_lo, s + 1)
                    else:
                        wait(pe, l.y_sb, s - 1)
                    o = ps[:, 2 + 2 * b + u, :]
                    bias(o, e * F + B_UP, F)
                    for c in range(KC):
                        ins = product(o, xT[0][:, b, u, c, :], xT[1][:, b, u, c, :],
                                      up_w[0][:, c, bass.ds(e, 1), :], up_w[1][:, c, bass.ds(e, 1), :], c == KC - 1)
                    ins.then_inc(l.gu, 1)

                def a_transpose(s, b):
                    pe.wait_ge(l.act, s + 1)
                    transpose4(6, act_v[:, b]).then_inc(l.a_T, 1)

                def down(s, e):
                    pe.wait_ge(l.a_lo, s + 1)
                    for u in range(2):
                        o = ps[:, 7, u * H:(u + 1) * H]
                        bias(o, e[u] * H + B_DN, H)
                        for c in range(KC):
                            ins = product(o, aT[0][:, u, c, :], aT[1][:, u, c, :],
                                          dn_w[0][:, c, bass.ds(e[u], 1), :], dn_w[1][:, c, bass.ds(e[u], 1), :],
                                          c == KC - 1)
                    ins.then_inc(l.y_ps, 1)

                x_transpose(0, 0, 0)
                x_transpose(1, 1, 0)
                load_names(0, 0)
                load_names(1, 1)
                e = named(0)
                for u in range(2):
                    up(0, 0, u, e[u])
                def body(it):
                    for d in range(2):
                        s, b = it * 2 + 1 + d, (1 + d) % 2
                        x_transpose(s + 1, 1 - b, it + 1)
                        e, e_last = named(b), named(1 - b)
                        up(s, b, 0, e[0])
                        load_names(s + 1, 1 - b)
                        a_transpose(s - 1, 1 - b)
                        up(s, b, 1, e[1])
                        down(s - 1, e_last)
                repeat(pe, NP // 2 - 1, body)
                e, e_last = named(1), named(0)
                up(NP - 1, 1, 0, e[0])
                a_transpose(NP - 2, 0)
                up(NP - 1, 1, 1, e[1])
                down(NP - 2, e_last)
                a_transpose(NP - 1, 1)
                pe.wait_ge(l.y_sb, NP - 1)
                down(NP - 1, e)

            layer_norm_loop(L[0])
            route(L[0])
            experts(L[0])

            def a_in(g, j):
                pe.wait_ge(A.xn, g + 1)
                transpose4(j % 2, xn_a[:, j]).then_inc(A.x_T, 1)

            def project(g, b):
                for u in range(2):
                    o = ps[:, 2 + 2 * b + u, :]
                    if u == 0:
                        pe.wait_ge(A.x_lo, g + 1)
                    bias(o, B_QK, 2 * H)
                    for c in range(KC):
                        ins = product(o, xT[0][:, b, u, c, :], xT[1][:, b, u, c, :], qk_w[0][:, c, :], qk_w[1][:, c, :],
                                      c == KC - 1)
                    ins.then_inc(qk_ps, 1)

            def key_sums(g, b, first=False, last=False):
                pe.wait_ge(k_lo, g + 1)
                for u in range(2):
                    for a in range(KC):
                        o = ps[:, 6 + a, 0:H + 2]
                        hi, lo = aT[0][:, u, a, :], aT[1][:, u, a, :]
                        nc.tensor.matmul(o, hi, xn1[0][:, b, u, :], start=first and u == 0, stop=False,
                                         skip_group_check=True)
                        nc.tensor.matmul(o, hi, xn1[1][:, b, u, :], start=False, stop=False, skip_group_check=True)
                        ins = nc.tensor.matmul(o, lo, xn1[0][:, b, u, :], start=False, stop=last and u == 1,
                                               skip_group_check=True)
                ins.then_inc(g_used, 1)

            def first_pass(g, j, it):
                static = isinstance(g, int)
                if not (static and not 1 <= g <= NG):
                    project(g - 1, (j + 1) % 2)
                if not (static and g >= NG):
                    a_in(g, j)
                if not (static and g < 3):
                    key_sums(g - 3, (j + 1) % 2, first=static and g == 3, last=static and g == NG + 2)
            stages(pe, first_pass)
            for g in range(NG, NG + 3):
                first_pass(g, g % 4, g // 4)

            def q_transpose(g, j, k):
                pe.wait_ge(q_loaded[j], 16 * (k + 1))
                transpose4(2 + j % 2, qin[:, j]).then_inc(q_T, 1)

            pe.wait_ge(out_w_loaded, 48)
            pe.wait_ge(mid_dve, 1)
            for c in range(KC):
                for a in range(KC):
                    nc.tensor.transpose(ps[:, 0, (c * KC + a) * P:(c * KC + a + 1) * P],
                                        gsb[:, a, c * P:(c + 1) * P], ident)
            for a in range(KC):
                ins = nc.tensor.transpose(ps[0:2, 1, a * P:(a + 1) * P], gsb[:, a, H:H + 2], ident)
            ins.then_inc(mid_pe, 1)
            q_transpose(0, 0, 0)
            pe.wait_ge(mid_dve, 2)
            for a in range(KC):
                o = ps[:, 5, a * P:(a + 1) * P]
                for c in range(KC):
                    nc.tensor.matmul(o, wv[:, c, a * P:(a + 1) * P], gT[:, c, a * P:(a + 1) * P],
                                     start=(c == 0), stop=False)
                ins = nc.tensor.matmul(o, bvrow[0:1, a * P:(a + 1) * P], ksT[0:1, a * P:(a + 1) * P],
                                       start=False, stop=True)
            ins.then_inc(mid_pe, 2)
            q_transpose(1, 1, 0)
            pe.wait_ge(mid_dve, 3)
            for a in range(KC):
                ins = nc.tensor.matmul(ps[:, 4, a * H:(a + 1) * H], sT[:, a, :], wo[:, a, :], start=True, stop=True)
            ins.then_inc(mid_pe, 1)

            def attend(g, b):
                for u in range(2):
                    o = ps[:, 4 + b, u * H:(u + 1) * H]
                    if u == 0:
                        wait(pe, x_done, g - 1)
                    bias(o, B_O, H)
                    if u == 0:
                        pe.wait_ge(q_lo, g + 1)
                    for a in range(KC):
                        ins = product(o, xT[0][:, b, u, a, :], xT[1][:, b, u, a, :], qk_w[0][:, a, 0:H],
                                      qk_w[1][:, a, 0:H], a == KC - 1)
                ins.then_inc(o_ps, 1)

            pe.wait_ge(m_lo, 1)
            attend(0, 0)
            q_transpose(2, 2, 0)
            attend(1, 1)
            l = L[1]

            def second_pass(g, j, it):
                b, static = j % 2, isinstance(g, int)
                if not (static and g + 3 >= NG):
                    q_transpose(g + 3, (j + 3) % 4, it + (j + 3) // 4)
                if not (static and g + 2 >= NG):
                    attend(g + 2, b)
                xn_transpose(l, g, b)
                if not (static and g < 1):
                    logits(l, g - 1, 1 - b)
            stages(pe, second_pass)
            logits(l, NG - 1, 1)
            route(l)
            experts(l)

        @block.vector
        def _(dve):
            v = nc.vector
            st = Steps(dve, dve_step, dve_passed)
            dve.wait_ge(consts_loaded, 16)
            v.memset(ones[:, :], 1.0)
            v.tensor_copy(upper[:, :], cst[:, C_UP:C_UP + P]).then_inc(consts_made, 1)

            def split_biases():
                dve.wait_ge(bias_loaded, 80)
                odd = bstage[:, 0:32].rearrange("p (f c) -> p f c", c=2)[:, :, 1]
                st.done(v.tensor_scalar(odd, odd, 1.0, None, ALU.add))
                st.done(v.tensor_copy(bparts[:, 0, :], bstage[:, :]))
                st.done(v.tensor_tensor(bres[:, :], bstage[:, :], bparts[:, 0, :], ALU.subtract))
                st.done(v.tensor_copy(bparts[:, 1, :], bres[:, :]))
                st.done(v.tensor_tensor(bres[:, :], bres[:, :], bparts[:, 1, :], ALU.subtract))
                v.tensor_copy(bparts[:, 2, :], bres[:, :]).then_inc(bias_split, 1)

            mv = [[sbmv[:, 4 * b + 2 * u:4 * b + 2 * u + 2] for u in range(2)] for b in range(2)]

            def moments(l, g, b):
                st.hold()
                for u in range(2):
                    ins = v.bn_stats(bst[:, u, :], xs[:, bass.ds(g * 2 + u, 1), :].rearrange("p a h -> p (a h)"))
                st.done(ins)
                st.hold()
                for u in range(2):
                    ins = v.bn_aggr(mv[b][u], bst[:, u, :])
                ins.then_inc(l.var, 1)

            def inverse(l, g, b):
                dve.wait_ge(l.sd, g + 1)
                return st.mark(v.reciprocal(small[:, 12 + 2 * b:14 + 2 * b], small[:, 8 + 2 * b:10 + 2 * b]))

            def normalise(l, dst, g, b, inverted):
                st.need(inverted)
                for u in range(2):
                    ins = v.tensor_scalar(dst[:, u, 0:H], xs[:, bass.ds(g * 2 + u, 1), :].rearrange("p a h -> p (a h)"),
                                          mv[b][u][:, 0:1], small[:, 12 + 2 * b + u:13 + 2 * b + u],
                                          ALU.subtract, ALU.mult)
                ins.then_inc(l.xn, 1)

            l = L[0]
            dve.wait_ge(x_loaded[0], 16)
            moments(l, 0, 0)

            def ln_step(g, j, it):
                b, static = j % 2, isinstance(g, int)
                if static and g == 3:
                    dve.wait_ge(x_loaded[1], 16)
                    split_biases()
                if j == 3 and not static:
                    for c in (2, 3):
                        dve.wait_ge(x_loaded[c], 16)
                k = it * 2 + j // 2
                wait(dve, l.xn_stored[b], 16 * k)
                normalise(l, xn_r[:, b], g, b, inverse(l, g, b))
                if not (static and g + 1 >= NG):
                    moments(l, g + 1, 1 - b)
            st.stages(8, ln_step)

            def route(n):
                l = L[n]
                mask = area(0, NT * E, dt=BF16)
                lg = logit[:, :, :]
                eq = area(6208, NT, E)
                cand = area(6608, NT, E)
                oh = [area(1024 + 256 * k, NT, E) for k in range(2)]
                prod = area(1536, NT, E)
                scan = [area(6208 + 400 * k, PAD + NT, E) for k in range(2)]
                top = area(7040, 2, NT)
                pick = area(7104, NT)
                pos = area(7136, NT, TOPK)
                posi = area(7200, 2, NQ, dt=I32)
                posb = area(7328, 2, NQ, dt=BF16)
                tiles = area(7400, 2, 16)
                tilei = area(7440, 16, dt=I32)
                nam = area(7460, 2, NS)
                cmp = area(512, NS, E)
                dve.wait_ge(l.logit_sb, NG)
                dve.wait_ge(iotas_made, n + 1)
                if n == 0:
                    dve.wait_ge(bias_stored, 16 * 5)
                eiota = cst[:, None, C_E:C_E + E].to_broadcast([P, NT, E])
                for k in range(TOPK):
                    st.done(v.tensor_reduce(top[:, k, :], lg, AX.X, ALU.max))
                    st.done(v.tensor_tensor(eq, lg, top[:, k, :, None].to_broadcast([P, NT, E]), ALU.is_equal))
                    st.done(v.scalar_tensor_tensor(out=cand, in0=eq, scalar=-float(E), in1=eiota,
                                                   op0=ALU.mult, op1=ALU.add))
                    st.done(v.tensor_reduce(pick, cand, AX.X, ALU.min))
                    st.done(v.tensor_tensor(oh[k], cand, pick[:, :, None].to_broadcast([P, NT, E]), ALU.is_equal))
                    if k == 0:
                        st.done(v.scalar_tensor_tensor(out=lg, in0=oh[0], scalar=MASKED, in1=lg,
                                                       op0=ALU.mult, op1=ALU.add))
                v.tensor_tensor(small[:, 16:16 + NT], top[:, 1, :], top[:, 0, :], ALU.subtract).then_inc(l.gap, 1)
                for b in range(2):
                    dve.wait_ge(l.xn_stored[b], 16 * (NG // 2))
                v.tensor_tensor(mask.rearrange("p (i e) -> p i e", e=E), oh[0], oh[1], ALU.add).then_inc(l.mask, 1)
                for k in range(2):
                    st.done(v.memset(scan[k][:, 0:PAD, :], 0.0))
                v.memset(tiles[:, :, 0:8], 0.0)
                dve.wait_ge(l.prefix, 1)
                st.done(v.tensor_copy(scan[0][:, PAD:, :],
                                      ps[:, 2, NT * E:2 * NT * E].rearrange("p (i e) -> p i e", e=E)))
                a = 0
                for d in (1, 2, 4, 8, 16):
                    st.done(v.tensor_tensor(scan[1 - a][:, PAD:, :], scan[a][:, PAD:, :],
                                            scan[a][:, PAD - d:PAD + NT - d, :], ALU.add))
                    a = 1 - a
                st.done(v.tensor_scalar(tilei[:, 0:E], scan[a][:, PAD + NT - 1, :], float(P - 1), None, ALU.add))
                st.done(v.tensor_single_scalar(tilei[:, 0:E], tilei[:, 0:E], 7, ALU.logical_shift_right))
                st.done(v.tensor_copy(tiles[:, 0, 8:16], tilei[:, 0:E]))
                c = 0
                for d in (1, 2, 4):
                    st.done(v.tensor_tensor(tiles[:, 1 - c, 8:16], tiles[:, c, 8:16], tiles[:, c, 8 - d:16 - d],
                                            ALU.add))
                    c = 1 - c
                before = tiles[:, c, 7:15]
                st.done(v.tensor_tensor(prod, ps[:, 2, 0:NT * E].rearrange("p (i e) -> p i e", e=E),
                                        scan[a][:, PAD - 1:PAD + NT - 1, :], ALU.add))
                st.done(v.scalar_tensor_tensor(out=prod, in0=before[:, None, :].to_broadcast([P, NT, E]), scalar=float(P),
                                               in1=prod, op0=ALU.mult, op1=ALU.add))
                for k in range(TOPK):
                    st.done(v.tensor_tensor(oh[k], oh[k], prod, ALU.mult))
                    st.done(v.tensor_reduce(pos[:, :, k], oh[k], AX.X, ALU.add))
                st.done(v.tensor_copy(posi[:, 1, :], pos.rearrange("p i k -> p (i k)")))
                st.done(v.tensor_single_scalar(posi[:, 0, :], posi[:, 1, :], 7, ALU.logical_shift_right))
                st.done(v.tensor_single_scalar(posi[:, 1, :], posi[:, 1, :], P - 1, ALU.bitwise_and))
                st.done(v.tensor_copy(posb, posi))
                row = slice(0, 1)
                st.done(v.tensor_tensor(cmp[row, :, 1:E], before[row, None, 1:E].to_broadcast([1, NS, E - 1]),
                                        iotaJ[row, :, 0:1].to_broadcast([1, NS, E - 1]), ALU.is_le))
                st.done(v.tensor_reduce(nam[row, 0, :], cmp[row, :, 1:E], AX.X, ALU.add))
                st.done(v.tensor_copy(expert[:, :], nam[row, 0, :]))
                if n == 0:
                    dve.wait_ge(raw_lo, E + 1)
                for ch in range(NQC):
                    if ch >= 2:
                        dve.wait_ge(l.hot_used, ch - 1)
                    hs, ht, low, _ = hot(ch % 2)
                    cols = slice(ch * QC, (ch + 1) * QC)
                    v.tensor_tensor(ht, iotaJ, posb[:, 0, None, cols].to_broadcast([P, NS, QC]),
                                    ALU.is_equal).then_inc(l.hot_tile, 1)
                    v.tensor_tensor(hs, iotaS, posb[:, 1, None, cols].to_broadcast([P, P, QC]), ALU.is_equal)
                    dve.wait_ge(l.hot_tile, ch + 1)
                    v.tensor_tensor(low, numbers[:, None, ch % 4 * QC:(ch % 4 + 1) * QC].to_broadcast([P, NS, QC]), ht, ALU.mult).then_inc(l.hot, 1)
                dve.wait_ge(l.hot_used, NQC)
                st.done(v.tensor_copy(nam[:, 1, :], ps[:, 3, 0:NS]))
                st.done(v.scalar_tensor_tensor(out=nam[:, 1, :], in0=ps[:, 4, 0:NS], scalar=32.0,
                                               in1=nam[:, 1, :], op0=ALU.mult, op1=ALU.add))
                st.done(v.tensor_scalar(nam[:, 0, :], nam[:, 1, :], 0.0, SKIP, ALU.is_equal, ALU.mult))
                v.scalar_tensor_tensor(out=sidx[:, :], in0=nam[:, 1, :], scalar=-1.0, in1=nam[:, 0, :],
                                       op0=ALU.add, op1=ALU.add)
                st.done(v.tensor_scalar(gidx[:, :], nam[:, 1, :], -1.0, 0.0, ALU.add, ALU.max))
                st.done(v.tensor_single_scalar(gidx[:, :], gidx[:, :], 1, ALU.logical_shift_right))
                dve.wait_ge(l.gates, 1)
                st.done(v.tensor_scalar(gate[:, :, :], gate[:, :, :], 0.5, None, ALU.mult))
                v.engine_nop().then_inc(l.routed, 1)

            def experts(l):
                def x_lo(s, b):
                    dve.wait_ge(l.x_hi, s + 1)
                    v.tensor_tensor(xT[1][:, b], ps[:, b, :].rearrange("p (u c t) -> p u c t", u=2, c=KC),
                                    xT[0][:, b].bitcast(F32), ALU.subtract).then_inc(l.x_lo, 1)

                def a_lo(s):
                    dve.wait_ge(l.a_hi, s + 1)
                    v.tensor_tensor(aT[1][:, :, :, :], ps[:, 6, :].rearrange("p (u c t) -> p u c t", u=2, c=KC),
                                    aT[0][:, :, :, :].bitcast(F32), ALU.subtract).then_inc(l.a_lo, 1)

                def activate(s, b):
                    for u in range(2):
                        dve.wait_ge(l.glu, s * 2 + u + 1)
                        ins = v.tensor_scalar(upv[:, u, :],
                                              ps[:, 2 + 2 * b + u, :].rearrange("p (f c) -> p f c", c=2)[:, :, 1],
                                              1.0 - LIMIT, 1.0 + LIMIT, ALU.max, ALU.min)
                    st.done(ins)
                    v.scalar_tensor_tensor(out=act_v[:, b], in0=glu[:, b], scalar=GLU_LIMIT, in1=upv[:, :, :],
                                           op0=ALU.min, op1=ALU.mult).then_inc(l.act, 1)

                x_lo(0, 0)
                x_lo(1, 1)
                activate(0, 0)

                def body(it):
                    for d in range(2):
                        s, b = it * 2 + 1 + d, (1 + d) % 2
                        x_lo(s + 1, 1 - b)
                        a_lo(s - 1)
                        activate(s, b)
                st.loop(NP // 2 - 1, 2, body)
                a_lo(NP - 2)
                activate(NP - 1, 1)
                a_lo(NP - 1)

            def combine(l, g, j, k, between=None):
                dve.wait_ge(l.y_loaded[j], 16 * (k + 1))

                def add(c):
                    for u in range(2):
                        xr = xs[:, bass.ds(g * 2 + u, 1), :].rearrange("p a h -> p (a h)")
                        ins = v.scalar_tensor_tensor(out=xr, in0=ybuf[:, j, u, c, :],
                                                     scalar=gate[:, c, bass.ds(g * 2 + u, 1)], in1=xr,
                                                     op0=ALU.mult, op1=ALU.add)
                    return ins
                first = st.mark(add(0))
                if between is not None:
                    between()
                st.need(first)
                add(1).then_inc(l.y_used, 1)

            route(0)
            experts(L[0])

            def xT_low(g, b):
                dve.wait_ge(A.x_hi, g + 1)
                v.tensor_tensor(xT[1][:, b], ps[:, b, :].rearrange("p (u c t) -> p u c t", u=2, c=KC),
                                xT[0][:, b].bitcast(F32), ALU.subtract).then_inc(A.x_lo, 1)

            def rotate(g, b):
                dve.wait_ge(qk_sb, g + 1)
                wait(dve, rot_done, g)
                for u in range(2):
                    w = qk[:, b, u, :].rearrange("p (h j c) -> p h j c", j=HD // 2, c=2)
                    sin = cst[:, bass.ds(g * 2 * ROT + (C_SIN + u * ROT), ROT)][:, None, :].to_broadcast(
                        [P, 2 * HEADS, ROT])
                    v.tensor_tensor(rotr[:, u], w[:, :, 0:ROT, 1], sin, ALU.mult)
                    ins = v.tensor_tensor(roti[:, u], w[:, :, 0:ROT, 0], sin, ALU.mult)
                ins.then_inc(rot_parts, 1)

            def first_pass(g, j, it):
                b, static = j % 2, isinstance(g, int)
                inverted = inverse(A, g, b)

                def turn_and_normalise():
                    if not (static and g < 2):
                        rotate(g - 2, b)
                    normalise(A, xn_a[:, j], g, b, inverted)
                if not (static and g == NG - 1):
                    combine(L[0], g + 1, 1 - b, it * 2 + (j + 1) // 2, turn_and_normalise)
                else:
                    turn_and_normalise()
                if not (static and g == NG - 1):
                    dve.wait_ge(L[0].y_used, g + 2)
                    moments(A, g + 1, 1 - b)
                xT_low(g, b)

            combine(L[0], 0, 0, 0)
            dve.wait_ge(L[0].y_used, 1)
            v.memset(xn1[0][:, :, :, H:H + 1].bitcast(F32), 1.0)
            v.memset(xn1[0][:, :, :, H + 1:H + 2].bitcast(F32), 0.0)
            v.memset(xn1[1][:, :, :, H:H + 2].bitcast(F32), 0.0)
            moments(A, 0, 0)
            st.stages(12, first_pass)
            rotate(NG - 2, 0)
            rotate(NG - 1, 1)

            def q_low(g, b):
                dve.wait_ge(q_hi, g + 1)
                v.tensor_tensor(xT[1][:, b], ps[:, 2 + b, :].rearrange("p (u c t) -> p u c t", u=2, c=KC),
                                xT[0][:, b].bitcast(F32), ALU.subtract).then_inc(q_lo, 1)

            dve.wait_ge(g_used, NG)
            v.tensor_copy(gsb, ps[:, 6:8, 0:H + 2]).then_inc(mid_dve, 1)
            dve.wait_ge(mid_pe, 1)
            v.tensor_copy(gT.rearrange("p c o -> p (c o)"), ps[:, 0, :])
            v.tensor_copy(ksT[0:1, :], ps[0:1, 1, 0:H]).then_inc(mid_dve, 1)
            q_low(0, 0)
            dve.wait_ge(mid_pe, 3)
            v.tensor_tensor(sT, ps[:, 5, 0:KC * P].rearrange("p (a k) -> p a k", a=KC),
                            cst[:, None, C_BLK:C_BLK + P].to_broadcast([P, KC, P]), ALU.mult).then_inc(mid_dve, 1)
            q_low(1, 1)
            dve.wait_ge(m_hi, 1)
            v.tensor_tensor(qk_w[1][:, :, 0:H], ps[:, 4, :].rearrange("p (a o) -> p a o", a=KC),
                            qk_w[0][:, :, 0:H].bitcast(F32), ALU.subtract).then_inc(m_lo, 1)
            dve.wait_ge(m_lo, 1)
            v.engine_nop().then_inc(mid_dve, 1)

            l1 = L[1]

            def add_out(g, b):
                dve.wait_ge(o_ps, g + 1)
                xr = pair(xs, g)
                v.tensor_tensor(xr, xr, ps[:, 4 + b, :].rearrange("p (u h) -> p u h", u=2), ALU.add).then_inc(x_done, 1)

            def second_pass(g, j, it):
                b, static = j % 2, isinstance(g, int)
                k = it * 2 + j // 2
                inverted = inverse(l1, g, b)
                if not (static and g + 1 >= NG):
                    add_out(g + 1, 1 - b)
                wait(dve, l1.xn_stored[b], 16 * k)
                normalise(l1, xn_r[:, b], g, b, inverted)
                if not (static and g + 1 >= NG):
                    dve.wait_ge(x_done, g + 2)
                    moments(l1, g + 1, 1 - b)
                if not (static and g + 3 >= NG):
                    q_low(g + 3, 1 - b)

            add_out(0, 0)
            dve.wait_ge(x_done, 1)
            moments(l1, 0, 0)
            q_low(2, 0)
            st.stages(8, second_pass)
            route(1)
            experts(l1)

            def last_body(it):
                for j in range(4):
                    combine(l1, it * 4 + j, j, it)
            st.loop(NG // 4, 4, last_body)


_INS = ["L0_attn_x", "L0_attn_Wq", "L0_attn_bq", "L0_attn_Wk", "L0_attn_bk", "L0_attn_Wv", "L0_attn_bv",
        "L0_attn_Wo", "L0_attn_bo", "L0_ffn_router_weight", "L0_ffn_gate_up_proj", "L0_ffn_gate_up_proj_bias",
        "L0_ffn_down_proj", "L0_ffn_down_proj_bias"]


def constants():
    import numpy as np
    c = np.zeros((P, NCONST), np.float32)
    c[:, C_ID:C_ID + P] = np.eye(P)
    c[:, C_UP:C_UP + P] = np.triu(np.ones((P, P)), 1)
    c[:, C_BLK:C_BLK + P] = np.kron(np.eye(P // HD), np.ones((HD, HD))) / np.sqrt(HD)
    freqs = np.zeros(ROT, np.float32)
    for j in range(ROT):
        freqs[j] = np.float32(1.0) / np.float32(10000.0 ** (2 * j))
    angles = np.arange(T, dtype=np.float32)[:, None] * freqs[None, :]
    c[:, C_COS:C_COS + NT] = np.cos(angles[:, 0]).reshape(P, NT)
    c[:, C_SIN:C_SIN + NT * ROT] = np.sin(angles).reshape(P, NT * ROT)
    for half in range(2):
        c[:, C_P + half] = 2 * np.arange(P) + half
    c[:, C_EPS] = EPS
    c[:, C_E:C_E + E] = np.arange(E)
    return c


def kernel(**inputs):
    import numpy as np
    import concourse.bacc as bacc
    from concourse.bass_utils import run_bass_kernel_spmd

    nc = bacc.Bacc("TRN2", target_bir_lowering=False, num_devices=1)
    arrays = {name: np.ascontiguousarray(inputs[name]) for name in _INS}
    arrays["constants"] = constants()
    args = [nc.dram_tensor(name, a.shape, mybir.dt.from_np(a.dtype), kind="ExternalInput").ap()
            for name, a in arrays.items()]
    out = nc.dram_tensor("out", (1, T, H), F32, kind="ExternalOutput").ap()
    build(nc, *args, out)
    r = run_bass_kernel_spmd(nc, [arrays], core_ids=[0])
    return r.results[0]["out"]
```
